# Optimizing a Trainium2 kernel written in Bass

```python
import numpy as np
import jax
import jax.numpy as jnp

def _softmax(x, axis=-1):
    return jax.nn.softmax(x, axis=axis)

def _gelu(x):
    return jax.nn.gelu(x, approximate=True)

def _silu(x):
    return jax.nn.silu(x)

def _sigmoid(x):
    return jax.nn.sigmoid(x)

def _layernorm(x, axis=-1, eps=1e-05):
    m = jnp.mean(x, axis=axis, keepdims=True)
    v = jnp.var(x, axis=axis, keepdims=True)
    return (x - m) / jnp.sqrt(v + eps)

def _scatter_add(tgt, idx, src, axis=0):
    return tgt.at[idx].add(src)

def _segment_sum(src, seg, n):
    return jax.ops.segment_sum(src, seg, n)
kernel_name = 'mk_xattn_ffn_d1_seqx_r4_c86462'

def setup_inputs(seed: int=0):
    np.random.seed(seed)
    _w = jnp.asarray

    def _rec_inputs():
        import jax
        import jax.numpy as jnp
        _rk = jax.random.key(seed)
        x = -0.0002928 + 1 * jax.random.normal(jax.random.fold_in(_rk, 1), (128, 128, 256), jnp.float32)
        _lenS = 128 - jax.random.randint(jax.random.fold_in(_rk, 7), (128,), 0, max(1, 128 // 4) + 1, jnp.int32)
        _lenS2 = 128 - jax.random.randint(jax.random.fold_in(_rk, 8), (128,), 0, max(1, 128 // 4) + 1, jnp.int32)
        _ctx_1024P = jax.random.normal(jax.random.fold_in(_rk, 11), (128, 16, 256), jnp.float32)
        _ctx_1024c = jax.random.dirichlet(jax.random.fold_in(_rk, 511), 0.3 * jnp.ones((16,), jnp.float32), (128, 128))
        _ctx_1024t = jnp.einsum('bsk,bkd->bsd', _ctx_1024c, _ctx_1024P)
        _ctx_1024t = _ctx_1024t * jax.lax.rsqrt(jnp.mean(jnp.square(_ctx_1024t)) + 1e-12) * 0.953939
        ctx_1024 = -1.39393e-06 + 0.999914 * (_ctx_1024t + 0.3 * jax.random.normal(jax.random.fold_in(_rk, 611), (128, 128, 256), jnp.float32))
        return (x, ctx_1024)
    x, ctx_1024 = _rec_inputs()

    def _L0_xattn_setup():
        import jax, jax.numpy as jnp
        import numpy as np
        B, T, D, H = (2, 512, 256, 16)
        DH = D // H
        key = jax.random.key(seed)
        ks = jax.random.split(key, 11)
        s = 1.0 / np.sqrt(D)
        return {'q': jax.random.normal(ks[0], (B, T, D), jnp.float32), 'k': jax.random.normal(ks[1], (B, T, D), jnp.float32), 'v': jax.random.normal(ks[2], (B, T, D), jnp.float32), 'wq_w': jax.random.normal(ks[3], (D, D), jnp.float32) * s, 'wq_b': jnp.zeros((D,), jnp.float32), 'wk_w': jax.random.normal(ks[4], (D, D), jnp.float32) * s, 'wk_b': jnp.zeros((D,), jnp.float32), 'wv_w': jax.random.normal(ks[5], (D, D), jnp.float32) * s, 'wv_b': jnp.zeros((D,), jnp.float32), 'wo_w': jax.random.normal(ks[6], (D, D), jnp.float32) * s, 'wo_b': jnp.zeros((D,), jnp.float32)}
    _L0_xattn_all = _L0_xattn_setup()
    _L0_xattn_in = {k: v for k, v in _L0_xattn_all.items() if k in ('wq_w', 'wq_b', 'wk_w', 'wk_b', 'wv_w', 'wv_b', 'wo_w', 'wo_b')}
    del _L0_xattn_all

    def _L0_ffn_setup():
        import jax, jax.numpy as jnp
        import numpy as np
        B, S, D = (2, 512, 256)
        I = 128
        E = 16
        TOP_K = 2

        def _mlp(x, wg, wu, wd):
            return jnp.einsum('bsi,id->bsd', jax.nn.silu(x @ wg) * (x @ wu), wd)
        key = jax.random.key(seed)
        ks = jax.random.split(key, 10)
        sc_d = 1.0 / np.sqrt(D)
        sc_i = 1.0 / np.sqrt(I)
        return {'x': jax.random.normal(ks[0], (B, S, D), dtype=jnp.float32), 'gate_w': jax.random.normal(ks[1], (D, E), dtype=jnp.float32) * sc_d, 'gate_b': jnp.zeros((E,), dtype=jnp.float32), 'shared_wg': jax.random.normal(ks[2], (D, I), dtype=jnp.float32) * sc_d, 'shared_wu': jax.random.normal(ks[3], (D, I), dtype=jnp.float32) * sc_d, 'shared_wd': jax.random.normal(ks[4], (I, D), dtype=jnp.float32) * sc_i, 'experts_wg': jax.random.normal(ks[5], (E, D, I), dtype=jnp.float32) * sc_d, 'experts_wu': jax.random.normal(ks[6], (E, D, I), dtype=jnp.float32) * sc_d, 'experts_wd': jax.random.normal(ks[7], (E, I, D), dtype=jnp.float32) * sc_i}
    _L0_ffn_all = _L0_ffn_setup()
    _L0_ffn_in = {k: v for k, v in _L0_ffn_all.items() if k in ('gate_w', 'gate_b', 'shared_wg', 'shared_wu', 'shared_wd', 'experts_wg', 'experts_wu', 'experts_wd')}
    del _L0_ffn_all
    return {'x': x, 'ctx_1024': ctx_1024, 'L0_xattn_wq_w': _L0_xattn_in['wq_w'], 'L0_xattn_wq_b': _L0_xattn_in['wq_b'], 'L0_xattn_wk_w': _L0_xattn_in['wk_w'], 'L0_xattn_wk_b': _L0_xattn_in['wk_b'], 'L0_xattn_wv_w': _L0_xattn_in['wv_w'], 'L0_xattn_wv_b': _L0_xattn_in['wv_b'], 'L0_xattn_wo_w': _L0_xattn_in['wo_w'], 'L0_xattn_wo_b': _L0_xattn_in['wo_b'], 'L0_ffn_gate_w': _L0_ffn_in['gate_w'], 'L0_ffn_gate_b': _L0_ffn_in['gate_b'], 'L0_ffn_shared_wg': _L0_ffn_in['shared_wg'], 'L0_ffn_shared_wu': _L0_ffn_in['shared_wu'], 'L0_ffn_shared_wd': _L0_ffn_in['shared_wd'], 'L0_ffn_experts_wg': _L0_ffn_in['experts_wg'], 'L0_ffn_experts_wu': _L0_ffn_in['experts_wu'], 'L0_ffn_experts_wd': _L0_ffn_in['experts_wd']}

def reference(x, ctx_1024, L0_xattn_wq_w, L0_xattn_wq_b, L0_xattn_wk_w, L0_xattn_wk_b, L0_xattn_wv_w, L0_xattn_wv_b, L0_xattn_wo_w, L0_xattn_wo_b, L0_ffn_gate_w, L0_ffn_gate_b, L0_ffn_shared_wg, L0_ffn_shared_wu, L0_ffn_shared_wd, L0_ffn_experts_wg, L0_ffn_experts_wu, L0_ffn_experts_wd):
    import jax
    import jax.numpy as jnp

    def _L0_xattn_ref(q, k, v, wq_w, wq_b, wk_w, wk_b, wv_w, wv_b, wo_w, wo_b):
        import jax, jax.numpy as jnp
        import numpy as np
        B, T, D, H = (2, 512, 256, 16)
        DH = D // H
        b, t, d = q.shape
        wq = (q @ wq_w.T + wq_b).reshape(b, t, H, DH)
        wk = (k @ wk_w.T + wk_b).reshape(b, t, H, DH)
        wv = (v @ wv_w.T + wv_b).reshape(b, t, H, DH)
        scores = jnp.einsum('bthd,bshd->bhts', wq, wk) / jnp.sqrt(jnp.float32(DH))
        probs = jax.nn.softmax(scores, axis=-1)
        attn = jnp.einsum('bhts,bshd->bthd', probs, wv)
        attn = attn.reshape(b, t, d)
        return attn @ wo_w.T + wo_b

    def _L0_ffn_ref(x, gate_w, gate_b, shared_wg, shared_wu, shared_wd, experts_wg, experts_wu, experts_wd):
        import jax, jax.numpy as jnp
        import numpy as np
        B, S, D = (2, 512, 256)
        I = 128
        E = 16
        TOP_K = 2

        def _mlp(x, wg, wu, wd):
            return jnp.einsum('bsi,id->bsd', jax.nn.silu(x @ wg) * (x @ wu), wd)
        router_logits = jax.nn.sigmoid(x @ gate_w + gate_b)
        expert_values, expert_indices = jax.lax.top_k(router_logits, k=TOP_K)
        expert_values = expert_values / jnp.sum(expert_values, axis=-1, keepdims=True)
        hg = jnp.einsum('bsd,edi->bsei', x, experts_wg)
        hu = jnp.einsum('bsd,edi->bsei', x, experts_wu)
        all_outputs = jnp.einsum('bsei,eid->bsed', jax.nn.silu(hg) * hu, experts_wd)
        selected = jnp.take_along_axis(all_outputs, expert_indices[..., None], axis=2)
        expert_weighted = jnp.sum(expert_values[..., None] * selected, axis=2)
        return x + _mlp(x, shared_wg, shared_wu, shared_wd) + expert_weighted
    x = x + _L0_xattn_ref(_layernorm(x, axis=-1), ctx_1024, ctx_1024, L0_xattn_wq_w, L0_xattn_wq_b, L0_xattn_wk_w, L0_xattn_wk_b, L0_xattn_wv_w, L0_xattn_wv_b, L0_xattn_wo_w, L0_xattn_wo_b)
    x = x + _L0_ffn_ref(_layernorm(x, axis=-1), L0_ffn_gate_w, L0_ffn_gate_b, L0_ffn_shared_wg, L0_ffn_shared_wu, L0_ffn_shared_wd, L0_ffn_experts_wg, L0_ffn_experts_wu, L0_ffn_experts_wd)
    return x

_drawn_inputs = setup_inputs


def setup_inputs(seed=0):
    import zlib

    import numpy as np

    out = dict(_drawn_inputs(seed))
    spreads = {'L0_xattn_wq_b': (0.0, 0.1),
     'L0_xattn_wk_b': (0.0, 0.1),
     'L0_xattn_wv_b': (0.0, 0.1),
     'L0_xattn_wo_b': (0.0, 0.1),
     'L0_ffn_gate_b': (0.0, 0.1)}
    factors = {}
    for name, (base, spread) in spreads.items():
        noise = np.random.default_rng([zlib.crc32(name.encode()), seed]).standard_normal(out[name].shape)
        drawn = base * np.exp(spread * noise) if base else spread * noise
        out[name] = jnp.asarray(drawn.astype(out[name].dtype))
    for name, factor in factors.items():
        out[name] = (out[name] * factor).astype(out[name].dtype)
    return out
```

```python
import concourse.bass as bass
from concourse import mybir
from contextlib import ExitStack

fp32 = mybir.dt.float32
fp16 = mybir.dt.float16
bf16 = mybir.dt.bfloat16
u32 = mybir.dt.uint32
i32 = mybir.dt.int32
ALU = mybir.AluOpType
ACT = mybir.ActivationFunctionType
AX = mybir.AxisListType

P = 128
H, DH = 16, 16
TOP_K = 2
LN_EPS = 1e-5
SIGMOID_ONE = 17.5


class Batch:

    def __init__(self, turn, offset, batches, unroll=2):
        self.turn, self.offset, self.batches, self.unroll = turn, offset, batches, unroll
        self.number = turn * unroll + offset
        self.slot = offset % 2
        self.slot4 = offset % 4

    def before(self, n):
        return Batch(self.turn, self.offset - n, self.batches, self.unroll)

    def exists(self):
        return not isinstance(self.number, int) or 0 <= self.number < self.batches


def after(engine, signal, batch, each=1, nth=None):
    if batch.exists():
        nth = each if nth is None else nth
        engine.wait_ge(signal, batch.turn * (batch.unroll * each) + batch.offset * each + nth)


def landed(engine, signals, batch):
    if batch.exists():
        n = len(signals)
        engine.wait_ge(signals[batch.offset % n],
                       batch.turn * (batch.unroll // n * 16) + (batch.offset // n + 1) * 16)


def after_first(engine, *events):
    for signal, batch in events:
        if batch.exists():
            after(engine, signal, batch)
            return


def for_all_steps(engine, batches, depth, step, unroll=2):
    peeled = 2 * unroll
    for i in range(peeled):
        step(Batch(0, i, batches, unroll))
    with engine.Fori(peeled // unroll, batches // unroll - 1) as turn:
        for u in range(unroll):
            step(Batch(turn, u, batches, unroll))
    for i in range(batches - unroll, batches + depth):
        step(Batch(0, i, batches, unroll))


def xattn_moe_kernel(nc, x, ctx_in, wq_t, wq_b, wk_t, wk_b, wv_t, wv_b, wo_t, wo_b,
                     gate_w, gate_b, shared_gu, shared_d, experts_gu, experts_d, out):
    TOKENS, D = x.shape
    BATCHES = TOKENS // P
    E = gate_w.shape[1]
    I = shared_d.shape[0]
    DC = D // P
    HC = 4
    REGION = TOKENS
    TILES = TOP_K * TOKENS // P + E

    TC = -(-TILES // P)
    TABLE_STEPS = 16

    xs_dram = nc.dram_tensor("expert_in", [E * REGION, D], fp32).ap()
    ys_dram = nc.dram_tensor("expert_out", [TILES * P, D], fp32).ap()
    base_dram = nc.dram_tensor("without_experts", [TOKENS, D], fp32).ap()

    with ExitStack() as stack:
        def sb(name, shape, dt=fp32):
            return stack.enter_context(nc.sbuf_tensor(name, shape, dt))

        def pb(name, shape, dt=fp32):
            return stack.enter_context(nc.psum_tensor(name, shape, dt))

        def sem(name):
            return stack.enter_context(nc.semaphore(name))

        wq_plain = sb("wq_plain", [P, DC, D])
        wk_plain = sb("wk_plain", [P, DC, D])
        wq_sb = sb("wq_sb", [P, DC, HC, P])
        wk_sb = sb("wk_sb", [P, DC, HC, P])
        wv_sb = sb("wv_sb", [P, DC, D])
        wo_sb = sb("wo_sb", [P, DC, D])
        gu_sb = sb("gu_sb", [P, DC, E + 2 * I])
        sd_sb = sb("sd_sb", [P, D])
        eg_sb = sb("eg_sb", [P, E, DC, 2 * I])
        ed_sb = sb("ed_sb", [P, E, D])
        bias_row = sb("bias_row", [1, 2, D])
        bias_rep = sb("bias_rep", [1, 2, HC * P])
        bias_left = sb("bias_left", [1, 2, HC * P])
        bias_parts = sb("bias_parts", [1, 3, 2, HC * P], bf16)
        bias3 = sb("bias3", [3, 2, HC * P], bf16)
        wo_b_row = sb("wo_b_row", [1, D])
        gate_b_row = sb("gate_b_row", [1, E])
        bv_col = sb("bv_col", [P, DC])
        bv_rep = sb("bv_rep", [P, DC, P])
        attn_bias = sb("attn_bias", [P, D])
        gate_bias = sb("gate_bias", [P, E])
        ones_row = sb("ones_row", [1, P])
        ones3 = sb("ones3", [3, P], bf16)
        ones_bf = sb("ones_bf", [P, P], bf16)
        col_iota = sb("col_iota", [P, P])
        row_int = sb("row_int", [P, 1], i32)
        row_int2 = sb("row_int2", [P, 2], i32)
        row_iota = sb("row_iota", [P, 1])
        row_mod4 = sb("row_mod4", [P, 1])
        low_half = sb("low_half", [P, 1])
        ident = sb("ident", [P, P])
        ident_bf = sb("ident_bf", [P, P], bf16)
        earlier = sb("earlier", [P, P], bf16)
        pick = sb("pick", [P, HC, P], bf16)
        minus_half = sb("minus_half", [P, 1])
        region_start = sb("region_start", [P, E])
        slot_all = sb("slot_all", [P, BATCHES, TOP_K])
        expert_all = sb("expert_all", [P, BATCHES, TOP_K])
        gate_all = sb("gate_all", [P, BATCHES, TOP_K])
        seen = sb("seen", [P, E], bf16)
        def two(name, shape, dt=fp32):
            return [sb(f"{name}{n}", shape, dt) for n in range(2)]

        spare_pool, spare_dve = two("spare_pool", [P, 1]), two("spare_dve", [P, 1])
        x_sb = two("x_sb", [P, D])
        c_sb = two("c_sb", [P, D])
        xn = two("xn", [P, D])
        x_res = two("x_res", [P, D])
        stats1, stats2 = two("stats1", [P, 6]), two("stats2", [P, 6])
        mv1, mv2 = two("mv1", [P, 2]), two("mv2", [P, 2])
        ve1, ve2 = two("ve1", [P, 1]), two("ve2", [P, 1])
        rstd1, rstd2 = two("rstd1", [P, 1]), two("rstd2", [P, 1])
        xc_t = two("xc_t", [P, 2 * DC, P])
        q_hi = two("q_hi", [P, HC * P], fp16)
        q_sb = two("q_sb", [P, HC, P], fp16)
        k_hi = two("k_hi", [P, HC, P], fp16)
        k_lo = two("k_lo", [P, HC, P], fp16)
        v_sb = two("v_sb", [P, H, 2 * DH])
        neg_max = two("neg_max", [P, 4, HC])
        max_parts = two("max_parts", [P, 4, 32], bf16)
        max_t = two("max_t", [P, P], bf16)
        probs = two("probs", [P, 4, HC, P])
        o_un = two("o_un", [P, HC, P])
        o_rec = two("o_rec", [P, HC, 4])
        o_sb = two("o_sb", [P, D])
        o_t = two("o_t", [P, DC, P])
        x1 = two("x1", [P, D])
        xn2 = two("xn2", [P, D])
        both = two("both", [P, D])
        xn2_t = two("xn2_t", [P, DC, P])
        key = two("key", [P, E])
        top_v = two("top_v", [P, 8])
        top_i = two("top_i", [P, 8], u32)
        chosen = two("chosen", [P, TOP_K, E])
        chosen_bf = two("chosen_bf", [P, E], bf16)
        rank = two("rank", [P, E])
        rank2 = two("rank2", [P, TOP_K, E])
        slot_int = two("slot_int", [P, TOP_K], u32)
        tanh_sb = two("tanh_sb", [P, I])
        act_g = two("act_g", [P, I])
        h_sb = two("h_sb", [P, I])
        h_t = two("h_t", [P, P])
        base_sb = two("base_sb", [P, D])

        rows_of = sb("rows_of", [P, E])
        count_int = sb("count_int", [P, E], i32)
        tiles_int = sb("tiles_int", [P, E], i32)
        tiles = sb("tiles", [P, E])
        tiles_end = sb("tiles_end", [P, E])
        final = sb("final", [P, E])
        full = sb("full", [P, E])
        back = sb("back", [P, E])
        edge = sb("edge", [P, 2, E + 1])
        jump = sb("jump", [P, 2, E + 1])
        out_shift = sb("out_shift", [P, E + 1])
        shift_part = sb("shift_part", [P, BATCHES * TOP_K])
        shifted = sb("shifted", [P, BATCHES * TOP_K])
        ones_e = sb("ones_e", [P, E])
        tile_iota = sb("tile_iota", [P, TC])
        last_tile = sb("last_tile", [P, 1])
        per_tile = sb("per_tile", [P, 3, TC, E])
        sums = sb("sums", [P, 3, TC])
        table_col = sb("table_col", [P, 2, TC])
        expert_tab = sb("expert_tab", [1, TC * P], i32)
        row_tab = sb("row_tab", [1, TC * P], i32)
        zeros = sb("zeros", [P, D])
        gate_sum = sb("gate_sum", [P, BATCHES])
        xe = [sb(f"xe{n}", [P, D]) for n in range(4)]
        xe_t = two("xe_t", [P, DC, P])
        te = two("te", [P, I])
        ge = two("ge", [P, I])
        he = two("he", [P, I])
        he_t = two("he_t", [P, P])
        ye = two("ye", [P, D])
        out_row = sb("out_row", [P, BATCHES * TOP_K], u32)
        gather_row = two("gather_row", [P, TOP_K], u32)
        first = two("first", [P, D])
        second = two("second", [P, D])
        rest = two("rest", [P, D])
        part = two("part", [P, D])
        total = two("total", [P, D])
        gates = two("gates", [P, TOP_K])

        ps_s = pb("ps_s", [P, 4, 512])
        b4, b5, b6, b7 = (pb(f"b{n}", [P, 512]) for n in (4, 5, 6, 7))
        ps_ot = b4[:, 0:D].rearrange("p (c t) -> p c t", c=DC)
        ps_xc = b5[:, :].rearrange("p (c t) -> p c t", c=2 * DC)
        ps_wo = b6[:, 0:D]
        ps_q = b7[:, :]
        ps_mt = b4[:, :].bitcast(bf16)[:, 0:P]
        ps_k = b5[:, :]
        ps_x2 = b6[:, 0:D].rearrange("p (c t) -> p c t", c=DC)
        ps_gu = b7[:, 0:E + 2 * I]
        ps_v = b4[:, 0:D]
        ps_rank = b5[:, 0:E]
        ps_pv = b6[:, :].rearrange("p (c t) -> p c t", c=HC)
        ps_h = b7[:, 0:P]
        ps_sd = b4[:, 0:D]
        ps_o = b5[:, :].rearrange("p (c r w) -> p c r w", c=HC, r=4)

        pe_xe = [ps_s[:, n, 0:D].rearrange("p (c t) -> p c t", c=DC) for n in range(2)]
        pe_gu = [ps_s[:, 2 + n, 0:2 * I] for n in range(2)]
        pe_h = [b4[:, 0:P], b5[:, 0:P]]
        pe_y = [b6[:, 0:D], b7[:, 0:D]]

        w_in, w_in2 = sem("w_in"), sem("w_in2")
        consts, bias_split, bias_in, setup_v, setup_pe, setup_done = (
            sem(n) for n in ("consts", "bias_split", "bias_in", "setup_v", "setup_pe", "setup_done"))
        setup_p = sem("setup_p")
        zeroed = sem("zeroed")
        x_in = [sem(f"x_in{n}") for n in range(2)]
        c_in = [sem(f"c_in{n}") for n in range(2)]
        base_out = [sem(f"base_out{n}") for n in range(2)]
        names = """stats1_done mv1_done ve1_done rstd1_done xn_done x_res_done
            xc_turned xc_kept q_made q_hi_done q_done k_made k_hi_done k_lo_done v_made v_done
            scores_made max_taken max_hi_done max_lo_done max_turned max_kept shifted_made
            probs_done pv_made pv_kept o_turned rec_done o_done
            ot_made ot_kept wo_made x1_done stats2_done mv2_done ve2_done rstd2_done xn2_done
            x2_turned x2_kept gu_made biased_done key_done topv_done topi_done expert_done
            chosen_done chosen_bf_done tanh_done gate_exp act_done h_done rank_made seen_done
            rank_done rank2_done slotf_done slot_done h_turned h_kept sd_made base_done
            both_done sent counted table tables_turned tables_kept shift_done gate_done
            xe_turned xe_kept ge_made te_done ge_done he_done he_turned he_kept ye_made ye_done
            gather_row_done gather_stood part_done gates_done total_done""".split()
        S = {n: sem(n) for n in names}
        xe_in = [sem(f"xe_in{n}") for n in range(4)]
        ye_out, first_in, second_in, rest_in, total_out = (
            [sem(f"{name}{n}") for n in range(2)]
            for name in ("ye_out", "first_in", "second_in", "rest_in", "total_out"))

        block = stack.enter_context(nc.Block())

        def rows(dram, batch):
            return dram[bass.ds(batch.number * P, P), :]

        @block.sync
        def _(sp):
            chunked = lambda w: w.rearrange("(c p) n -> p c n", p=P)
            for dst, src in ((wq_plain[:], chunked(wq_t)), (wk_plain[:], chunked(wk_t)),
                             (bias_row[:, 0, :], wq_b), (bias_row[:, 1, :], wk_b),
                             (wv_sb[:], chunked(wv_t)), (wo_sb[:], chunked(wo_t)),
                             (bv_col[:], wv_b), (wo_b_row[:], wo_b), (gate_b_row[:], gate_b),
                             (gu_sb[:, :, 0:E], chunked(gate_w)),
                             (gu_sb[:, :, E:E + 2 * I], chunked(shared_gu)), (sd_sb[:], shared_d)):
                sp.dma_start(dst, src).then_inc(w_in, 16)
            for b in range(2):
                sp.dma_start(x_sb[b][:], x[b * P:(b + 1) * P, :]).then_inc(x_in[b], 16)
            sp.dma_start(c_sb[0][:], ctx_in[0:P, :]).then_inc(c_in[0], 16)
            sp.wait_ge(consts, 2)
            for e in range(E):
                sp.dma_start(xs_dram[e * REGION:e * REGION + P, :], zeros[:]).then_inc(zeroed, 16)
            sp.wait_ge(bias_split, 5)
            for n in range(3):
                sp.dma_start(bias3[n:n + 1, :, :], bias_parts[:, n, :, :]).then_inc(bias_in, 16)
            sp.dma_start(eg_sb[:], experts_gu.rearrange("e (c p) n -> p e c n", p=P)).then_inc(w_in2, 16)
            sp.dma_start(ed_sb[:], experts_d.rearrange("e p n -> p e n")).then_inc(w_in2, 16)

            def step(i):
                b = i.before(-1)
                if b.exists():
                    after(sp, S["xc_turned"], b.before(2))
                    sp.dma_start(c_sb[b.slot][:], rows(ctx_in, b)).then_inc(c_in[b.slot], 16)
                b = i.before(2)
                if b.exists():
                    after(sp, S["base_done"], b)
                    sp.dma_start(rows(base_dram, b), base_sb[b.slot][:]).then_inc(base_out[b.slot], 16)
                b = i.before(-2)
                if b.exists():
                    after(sp, S["x_res_done"], i)
                    after(sp, S["xn_done"], i)
                    sp.dma_start(x_sb[b.slot][:], rows(x, b)).then_inc(x_in[b.slot], 16)

            for_all_steps(sp, BATCHES, 2, step)

            for n in range(2):
                sp.wait_ge(base_out[n], BATCHES // 2 * 16)
            sp.wait_ge(S["sent"], 32 * BATCHES)
            sp.wait_ge(S["tables_kept"], 2)

            def tile_step(i):
                if i.exists():
                    after(sp, S["xe_turned"], i.before(4))
                    row = sp.value_load(row_tab[0:1, bass.ds(i.number, 1)], min_val=0,
                                        max_val=E * REGION - P)
                    sp.dma_start(xe[i.slot4][:], xs_dram[bass.ds(row, P), :]).then_inc(xe_in[i.slot4], 16)
                o = i.before(6)
                if o.exists():
                    after(sp, S["ye_done"], o)
                    sp.dma_start(rows(ys_dram, o), ye[o.slot][:]).then_inc(ye_out[o.slot], 16)

            for_all_steps(sp, TILES, 6, tile_step, 4)

            def last_step(i):
                if i.exists():
                    after(sp, S["part_done"], i.before(2))
                    sp.dma_start(rest[i.slot][:], rows(base_dram, i)).then_inc(rest_in[i.slot], 16)
                o = i.before(1)
                if o.exists():
                    after(sp, S["total_done"], o)
                    sp.dma_start(rows(out, o), total[o.slot][:]).then_inc(total_out[o.slot], 16)

            for_all_steps(sp, BATCHES, 1, last_step)
            for n in range(2):
                sp.wait_ge(total_out[n], BATCHES // 2 * 16)

        @block.gpsimd
        def _(pool):
            g = nc.gpsimd

            def stand(b, signal):
                after(pool, signal, b.before(2))
                g.tensor_tensor(spare_pool[b.slot][:], minus_half[:], minus_half[:],
                                ALU.add).then_inc(signal, 1)

            g.iota(col_iota[:], pattern=[[1, P]], base=0, channel_multiplier=0,
                   allow_small_or_imprecise_dtypes=True)
            g.iota(row_int[:], pattern=[[0, 1]], base=0, channel_multiplier=1)
            g.iota(region_start[:], pattern=[[REGION, E]], base=0, channel_multiplier=0,
                   allow_small_or_imprecise_dtypes=True)
            g.memset(minus_half[:], -0.5)
            g.memset(ones_row[:], 1.0)
            g.memset(ones3[:], 1.0)
            g.memset(ones_bf[:], 1.0)
            g.memset(seen[:], 0.0)
            for n in range(2):
                g.memset(v_sb[n][:, :, DH:DH + 1], 1.0)
                g.memset(v_sb[n][:, :, DH + 1:], 0.0)
                g.memset(max_parts[n][:], 0.0)
            g.memset(probs[0][:, 0, 0, 0:1], 0.0).then_inc(consts, 1)
            g.iota(tile_iota[:], pattern=[[P, TC]], base=0, channel_multiplier=1,
                   allow_small_or_imprecise_dtypes=True)
            g.memset(zeros[:], 0.0)
            g.memset(ones_e[:], 1.0).then_inc(consts, 1)
            pool.wait_ge(consts, 2)

            def norm_pow(b, source, target, ready, free, done):
                after(pool, ready, b)
                after(pool, free, b.before(2))
                g.tensor_tensor(target[b.slot][:], source[b.slot][:], minus_half[:],
                                ALU.pow).then_inc(done, 1)

            def scatter_free(b, k):
                if k == 0 and isinstance(b.number, int) and b.number == 0:
                    pool.wait_ge(zeroed, 16 * E)
                after(pool, S["slot_done"], b)
                if k:
                    after(pool, S["sent"], b, 32, 16)
                else:
                    after(pool, S["sent"], b.before(1), 32)

            def scatter(b, k):
                g.indirect_dma_start(
                    xs_dram[:, :], bass.IndirectOffsetOnAxis(ap=slot_int[b.slot][:, k:k + 1], axis=0),
                    xn2[b.slot][:], None).then_inc(S["sent"], 16)

            norm_pow(Batch(0, 0, BATCHES), ve1, rstd1, S["ve1_done"], S["xn_done"], S["rstd1_done"])

            def step(i):
                b = i.before(2)
                if b.exists():
                    norm_pow(b, ve2, rstd2, S["ve2_done"], S["xn2_done"], S["rstd2_done"])
                b = i.before(-1)
                if b.exists():
                    norm_pow(b, ve1, rstd1, S["ve1_done"], S["xn_done"], S["rstd1_done"])
                b = i.before(3)
                if b.exists():
                    scatter_free(b, 1)
                if i.exists():
                    if isinstance(i.number, int) and i.number == 0:
                        pool.wait_ge(setup_done, 1)
                    landed(pool, x_in, i)
                    after(pool, S["x1_done"], i.before(2))
                    g.tensor_tensor(x_res[i.slot][:], x_sb[i.slot][:], attn_bias[:],
                                    ALU.add).then_inc(S["x_res_done"], 1)
                if b.exists():
                    scatter(b, 1)
                b = i.before(2)
                if b.exists():
                    after(pool, S["xn2_done"], b)
                    after(pool, S["base_done"], b.before(2))
                    g.tensor_tensor(both[b.slot][:], x1[b.slot][:], xn2[b.slot][:],
                                    ALU.add).then_inc(S["both_done"], 1)
                    scatter_free(b, 0)
                    after(pool, S["rank_made"], b)
                    after(pool, S["seen_done"], b.before(1))
                    g.tensor_tensor(seen[:], seen[:], chosen_bf[b.slot][:],
                                    ALU.add).then_inc(S["seen_done"], 1)
                    scatter(b, 0)

            for_all_steps(pool, BATCHES, 2, step)
            scatter_free(Batch(0, BATCHES - 1, BATCHES), 1)
            scatter(Batch(0, BATCHES - 1, BATCHES), 1)

            pool.wait_ge(S["shift_done"], 4 * E + 2)
            for n in range(2):
                pool.wait_ge(ye_out[n], TILES // 2 * 16)

            def last_step(i):
                if not i.exists():
                    return
                landed(pool, first_in, i.before(2))
                landed(pool, second_in, i.before(2))
                g.tensor_copy(gather_row[i.slot][:], out_row[:, bass.ds(i.number * TOP_K, TOP_K)]
                              ).then_inc(S["gather_row_done"], 1)
                after(pool, S["gather_row_done"], i)
                after(pool, S["total_done"], i.before(2))
                stand(i, S["gather_stood"])
                for k, (dst, signal) in enumerate(((first, first_in), (second, second_in))):
                    g.indirect_dma_start(dst[i.slot][:], None, ys_dram[:, :], bass.IndirectOffsetOnAxis(
                        ap=gather_row[i.slot][:, k:k + 1], axis=0)).then_inc(signal[i.slot], 16)

            for_all_steps(pool, BATCHES, 0, last_step)

        @block.scalar
        def _(act):
            a = nc.scalar
            def copy(dst, src):
                return a.activation(dst, src, ACT.Copy)

            act.wait_ge(setup_v, 1)

            def step(i):
                s, o = i.before(1), i.before(2)
                if o.exists():
                    after(act, S["ot_made"], o)
                    after(act, S["wo_made"], o.before(2))
                    copy(o_t[o.slot][:], ps_ot).then_inc(S["ot_kept"], 1)
                if i.exists():
                    after(act, S["xc_turned"], i)
                    after(act, S["v_made"], i.before(2))
                    copy(xc_t[i.slot][:], ps_xc).then_inc(S["xc_kept"], 1)
                    after(act, S["q_made"], i)
                    after(act, S["q_done"], i.before(2))
                    a.activation(q_hi[i.slot][:], ps_q, ACT.Identity, scale=low_half[:, 0:1]
                                 ).then_inc(S["q_hi_done"], 1)
                if s.exists():
                    after(act, S["max_turned"], s)
                    after(act, S["shifted_made"], s.before(2), 4)
                    copy(max_t[s.slot][:], ps_mt).then_inc(S["max_kept"], 1)
                if i.exists():
                    after(act, S["k_made"], i)
                    after(act, S["shifted_made"], i.before(2), 4)
                    copy(k_hi[i.slot][:].rearrange("p c t -> p (c t)"), ps_k).then_inc(S["k_hi_done"], 1)
                if o.exists():
                    after(act, S["x2_turned"], o)
                    after(act, S["gu_made"], o.before(2))
                    copy(xn2_t[o.slot][:], ps_x2).then_inc(S["x2_kept"], 1)

                def exps(r):
                    after(act, S["shifted_made"], s, 4, r + 1)
                    after(act, S["pv_made"], s.before(2))
                    a.activation(probs[s.slot][:, r, :, :], ps_s[:, r, :].rearrange("p (c t) -> p c t", c=HC),
                                 ACT.Exp, scale=DH ** -0.5).then_inc(S["probs_done"], 1)

                if s.exists():
                    exps(0)
                    exps(1)
                if o.exists():
                    after(act, S["biased_done"], o)
                    after(act, S["act_done"], o.before(2))
                    a.activation(tanh_sb[o.slot][:], ps_gu[:, E:E + I], ACT.Tanh, scale=0.5
                                 ).then_inc(S["tanh_done"], 1)
                if s.exists():
                    exps(2)
                    exps(3)
                if i.exists():
                    after(act, S["v_made"], i)
                    after(act, S["pv_made"], i.before(2))
                    copy(v_sb[i.slot][:, :, 0:DH], ps_v.rearrange("p (h w) -> p h w", h=H)
                         ).then_inc(S["v_done"], 1)
                if o.exists():
                    after(act, S["topv_done"], o)
                    a.activation(gate_all[:, bass.ds(o.number, 1), :], top_v[o.slot][:, 0:TOP_K].rearrange("p (a b) -> p a b", a=1),
                                 ACT.Exp, scale=-1.0).then_inc(S["gate_exp"], 1)
                if s.exists():
                    after(act, S["pv_made"], s)
                    after(act, S["o_turned"], s.before(2))
                    copy(o_un[s.slot][:], ps_pv).then_inc(S["pv_kept"], 1)
                if o.exists():
                    after(act, S["h_turned"], o)
                    after(act, S["sd_made"], o.before(2))
                    copy(h_t[o.slot][:], ps_h).then_inc(S["h_kept"], 1)

            for_all_steps(act, BATCHES, 2, step)

            def tile_step(i):
                t, h = i.before(1), i.before(2)
                if i.exists():
                    after(act, S["xe_turned"], i)
                    after(act, S["ge_made"], i.before(2))
                    copy(xe_t[i.slot][:], pe_xe[i.slot]).then_inc(S["xe_kept"], 1)
                if t.exists():
                    after(act, S["ge_made"], t)
                    after(act, S["ge_done"], t.before(2))
                    a.activation(te[t.slot][:], pe_gu[t.slot][:, 0:I], ACT.Tanh, scale=0.5
                                 ).then_inc(S["te_done"], 1)

            for_all_steps(act, TILES, 3, tile_step, 4)

        @block.vector
        def _(dve):
            v = nc.vector

            def stand(slot):
                v.memset(spare_dve[slot][:], 0.0)


            dve.wait_ge(consts, 1)
            v.tensor_copy(row_iota[:], row_int[:])
            v.tensor_scalar(row_int2[:, 0:1], row_int[:], 3, None, ALU.bitwise_and)
            v.tensor_scalar(row_int2[:, 1:2], row_int[:], 4, 1, ALU.logical_shift_right,
                            ALU.bitwise_and).then_inc(setup_v, 1)
            dve.wait_ge(setup_v, 1)
            v.tensor_copy(row_mod4[:], row_int2[:, 0:1])
            v.tensor_copy(low_half[:], row_int2[:, 1:2])
            v.tensor_scalar(ident[:], col_iota[:], row_iota[:, 0:1], None, ALU.is_equal)
            v.tensor_scalar(ident_bf[:], col_iota[:], row_iota[:, 0:1], None, ALU.is_equal)
            v.tensor_scalar(earlier[:], col_iota[:], row_iota[:, 0:1], None,
                            ALU.is_gt).then_inc(setup_v, 1)
            dve.wait_ge(setup_v, 2)
            for c in range(HC):
                v.tensor_scalar(pick[:, c, :], row_mod4[:, 0:1].to_broadcast([P, P]), float(c),
                                None, ALU.is_equal)
            dve.wait_ge(w_in, 16 * 12)
            rep = lambda t: t.rearrange("p c (h w) -> p c h w", w=DH).unsqueeze(3).to_broadcast([P, DC, H, 2, DH])
            for wide, plain in ((wq_sb, wq_plain), (wk_sb, wk_plain)):
                for c in range(DC):
                    dst = wide[:, c, :, :].rearrange("p g (r k w) -> p (g r) k w", k=2, w=DH)
                    for k in range(2):
                        v.tensor_copy(dst[:, :, k, :], plain[:, c, :].rearrange("p (h w) -> p h w", w=DH))
            v.tensor_copy(bv_rep[:], bv_col[:, :].unsqueeze(2).to_broadcast([P, DC, P]))
            for n in range(2):
                for k in range(2):
                    v.tensor_copy(bias_rep[:, n, :].rearrange("p (h k w) -> p h k w", k=2, w=DH)[:, :, k, :],
                                  bias_row[:, n, :].rearrange("p (h w) -> p h w", w=DH)
                                  ).then_inc(setup_p, 1)
            dve.wait_ge(setup_p, 4)
            v.tensor_copy(bias_parts[:, 0], bias_rep[:]).then_inc(bias_split, 1)
            dve.wait_ge(bias_split, 1)
            v.tensor_tensor(bias_left[:], bias_rep[:], bias_parts[:, 0], ALU.subtract).then_inc(bias_split, 1)
            dve.wait_ge(bias_split, 2)
            v.tensor_copy(bias_parts[:, 1], bias_left[:]).then_inc(bias_split, 1)
            dve.wait_ge(bias_split, 3)
            v.tensor_tensor(bias_rep[:], bias_left[:], bias_parts[:, 1], ALU.subtract).then_inc(bias_split, 1)
            dve.wait_ge(bias_split, 4)
            v.tensor_copy(bias_parts[:, 2], bias_rep[:]).then_inc(bias_split, 1)
            dve.wait_ge(setup_pe, 1)
            v.tensor_copy(attn_bias[:], b4[:, 0:D])
            v.tensor_copy(gate_bias[:], b5[:, 0:E]).then_inc(setup_done, 1)

            def stats_of(b, source, ready, stats, mv, ve, sems, free_mv, free_ve):
                if isinstance(ready, list):
                    landed(dve, ready, b)
                else:
                    after(dve, ready, b)
                v.bn_stats(stats[b.slot][:], source[b.slot][:]).then_inc(S[sems[0]], 1)
                after(dve, S[sems[0]], b)
                after(dve, free_mv, b.before(2))
                stand(b.slot)
                v.bn_aggr(mv[b.slot][:], stats[b.slot][:]).then_inc(S[sems[1]], 1)
                after(dve, S[sems[1]], b)
                after(dve, free_ve, b.before(2))
                v.tensor_scalar_add(ve[b.slot][:], mv[b.slot][:, 1:2], LN_EPS).then_inc(S[sems[2]], 1)

            def normalise(b, source, target, mv, rstd, ready, done, free, each=1):
                after(dve, ready, b)
                after(dve, free, b.before(2), each)
                v.tensor_scalar(target[b.slot][:], source[b.slot][:], mv[b.slot][:, 0:1],
                                rstd[b.slot][:, 0:1], ALU.subtract, ALU.mult).then_inc(done, 1)

            def stats_x(b):
                stats_of(b, x_sb, x_in, stats1, mv1, ve1, ("stats1_done", "mv1_done", "ve1_done"),
                         S["xn_done"], S["rstd1_done"])

            def normalise_x(b):
                normalise(b, x_sb, xn, mv1, rstd1, S["rstd1_done"], S["xn_done"], S["xc_turned"])

            stats_x(Batch(0, 0, BATCHES))
            normalise_x(Batch(0, 0, BATCHES))

            def step(i):
                s, o, n = i.before(1), i.before(2), i.before(-1)
                if s.exists():
                    for r in range(4):
                        after(dve, S["scores_made"], s, 4, r + 1)
                        after(dve, S["max_lo_done"], s.before(2))
                        v.tensor_reduce(neg_max[s.slot][:, r, :], ps_s[:, r, :].rearrange("p (c t) -> p c t", c=HC),
                                        axis=AX.X, op=ALU.max, negate=True).then_inc(S["max_taken"], 1)
                    after(dve, S["max_taken"], s, 4)
                    after(dve, S["max_turned"], s.before(2))
                    v.tensor_copy(max_parts[s.slot][:, :, 0:HC], neg_max[s.slot][:]).then_inc(S["max_hi_done"], 1)
                    after(dve, S["max_hi_done"], s)
                    v.tensor_tensor(max_parts[s.slot][:, :, HC:2 * HC], neg_max[s.slot][:],
                                    max_parts[s.slot][:, :, 0:HC], ALU.subtract).then_inc(S["max_lo_done"], 1)
                if o.exists():
                    after(dve, S["wo_made"], o)
                    after(dve, S["x_res_done"], o)
                    after(dve, S["base_done"], o.before(2))
                    v.tensor_tensor(x1[o.slot][:], ps_wo, x_res[o.slot][:], ALU.add).then_inc(S["x1_done"], 1)
                    stats_of(o, x1, S["x1_done"], stats2, mv2, ve2,
                             ("stats2_done", "mv2_done", "ve2_done"), S["xn2_done"], S["rstd2_done"])
                if i.exists():
                    after(dve, S["q_hi_done"], i)
                    after(dve, S["shifted_made"], i.before(2), 4)
                    v.tensor_tensor(q_sb[i.slot][:].rearrange("p c t -> p (c t)"), ps_q, q_hi[i.slot][:],
                                    ALU.subtract).then_inc(S["q_done"], 1)
                if o.exists():
                    normalise(o, x1, xn2, mv2, rstd2, S["rstd2_done"], S["xn2_done"], S["sent"], 32)
                if n.exists():
                    stats_x(n)
                if i.exists():
                    after(dve, S["k_hi_done"], i)
                    after(dve, S["shifted_made"], i.before(2), 4)
                    v.tensor_tensor(k_lo[i.slot][:].rearrange("p c t -> p (c t)"), ps_k,
                                    k_hi[i.slot][:].rearrange("p c t -> p (c t)"),
                                    ALU.subtract).then_inc(S["k_lo_done"], 1)
                if n.exists():
                    normalise_x(n)
                if o.exists():
                    after(dve, S["gu_made"], o)
                    after(dve, S["key_done"], o.before(1))
                    v.tensor_tensor(key[o.slot][:], ps_gu[:, 0:E], gate_bias[:], ALU.add).then_inc(S["biased_done"], 1)
                    after(dve, S["biased_done"], o)
                    v.tensor_scalar_min(key[o.slot][:], key[o.slot][:], SIGMOID_ONE).then_inc(S["key_done"], 1)
                    after(dve, S["key_done"], o)
                    after(dve, S["gate_exp"], o.before(2))
                    stand(o.slot)
                    v.max(top_v[o.slot][:], key[o.slot][:]).then_inc(S["topv_done"], 1)
                    after(dve, S["topv_done"], o)
                    stand(o.slot)
                    v.max_index(top_i[o.slot][:], top_v[o.slot][:], key[o.slot][:]).then_inc(S["topi_done"], 1)
                    after(dve, S["topi_done"], o)
                    stand(o.slot)
                    v.tensor_copy(expert_all[:, bass.ds(o.number, 1), :].rearrange("p a b -> p (a b)"),
                                  top_i[o.slot][:, 0:TOP_K]).then_inc(S["expert_done"], 1)
                    after(dve, S["expert_done"], o)
                    v.tensor_tensor(chosen[o.slot][:], col_iota[:, 0:E].unsqueeze(1).to_broadcast([P, TOP_K, E]),
                                    expert_all[:, bass.ds(o.number, 1), :].rearrange("p a b -> p (a b)").unsqueeze(2).to_broadcast([P, TOP_K, E]),
                                    ALU.is_equal).then_inc(S["chosen_done"], 1)
                    after(dve, S["chosen_done"], o)
                    after(dve, S["seen_done"], o.before(2))
                    v.tensor_tensor(chosen_bf[o.slot][:], chosen[o.slot][:, 0, :], chosen[o.slot][:, 1, :],
                                    ALU.add).then_inc(S["chosen_bf_done"], 1)
                    after(dve, S["tanh_done"], o)
                    v.scalar_tensor_tensor(act_g[o.slot][:], tanh_sb[o.slot][:], 1.0, ps_gu[:, E:E + I],
                                           ALU.add, ALU.mult).then_inc(S["act_done"], 1)
                    after(dve, S["act_done"], o)
                    after(dve, S["h_turned"], o.before(2))
                    v.scalar_tensor_tensor(h_sb[o.slot][:], act_g[o.slot][:], 0.5, ps_gu[:, E + I:E + 2 * I],
                                           ALU.mult, ALU.mult).then_inc(S["h_done"], 1)
                    after(dve, S["rank_made"], o)
                    v.tensor_tensor(rank[o.slot][:], ps_rank, region_start[:], ALU.add).then_inc(S["rank_done"], 1)
                    after(dve, S["rank_done"], o)
                    v.tensor_tensor(rank2[o.slot][:], chosen[o.slot][:],
                                    rank[o.slot][:, :].unsqueeze(1).to_broadcast([P, TOP_K, E]),
                                    ALU.mult).then_inc(S["rank2_done"], 1)
                    after(dve, S["rank2_done"], o)
                    v.tensor_reduce(slot_all[:, bass.ds(o.number, 1), :].rearrange("p a b -> p (a b)"), rank2[o.slot][:],
                                    axis=AX.X, op=ALU.add).then_inc(S["slotf_done"], 1)
                    after(dve, S["slotf_done"], o)
                    after(dve, S["sent"], o.before(2), 32)
                    stand(o.slot)
                    v.tensor_copy(slot_int[o.slot][:], slot_all[:, bass.ds(o.number, 1), :].rearrange("p a b -> p (a b)")
                                  ).then_inc(S["slot_done"], 1)
                    after(dve, S["sd_made"], o)
                    after(dve, S["both_done"], o)
                    landed(dve, base_out, o.before(2))
                    v.tensor_tensor(base_sb[o.slot][:], ps_sd, both[o.slot][:], ALU.add).then_inc(S["base_done"], 1)
                if s.exists():
                    after(dve, S["o_turned"], s)
                    after(dve, S["o_done"], s.before(2))
                    v.reciprocal(o_rec[s.slot][:], ps_o[:, :, :, DH]).then_inc(S["rec_done"], 1)
                    after(dve, S["rec_done"], s)
                    after(dve, S["ot_made"], s.before(2))
                    v.tensor_tensor(o_sb[s.slot][:].rearrange("p (c r w) -> p c r w", c=HC, r=4),
                                    ps_o[:, :, :, 0:DH], o_rec[s.slot][:].unsqueeze(3).to_broadcast([P, HC, 4, DH]),
                                    ALU.mult).then_inc(S["o_done"], 1)

            for_all_steps(dve, BATCHES, 2, step)

            def link(instruction):
                instruction.then_inc(S["table"], 1)
                table[0] += 1
                dve.wait_ge(S["table"], table[0])

            table = [0]
            dve.wait_ge(consts, 2)
            dve.wait_ge(S["counted"], 1)
            across = lambda t: t.unsqueeze(1).to_broadcast([P, TC, E])
            along = lambda t: t.unsqueeze(2).to_broadcast([P, TC, E])
            link(v.tensor_copy(rows_of[:], b5[:, 0:E]))
            link(v.tensor_scalar_add(count_int[:], rows_of[:], float(P - 1)))
            link(v.tensor_scalar(tiles_int[:], count_int[:], P.bit_length() - 1, None, ALU.logical_shift_right))
            link(v.tensor_copy(tiles[:], tiles_int[:]))
            link(v.tensor_tensor_scan(tiles_end[:], ones_e[:], tiles[:], 0.0, ALU.mult, ALU.add))
            v.tensor_scalar_add(final[:], tiles_end[:], -1.0)
            v.tensor_scalar(full[:], rows_of[:], float(P), None, ALU.is_ge)
            link(v.tensor_scalar_add(last_tile[:], tiles_end[:, E - 1:E], -1.0))
            link(v.scalar_tensor_tensor(back[:], tiles[:], float(P), rows_of[:], ALU.mult, ALU.subtract))
            link(v.tensor_tensor(back[:], back[:], full[:], ALU.mult))
            link(v.tensor_scalar(tile_iota[:], tile_iota[:], last_tile[:, 0:1], None, ALU.min))
            link(v.tensor_tensor(per_tile[:, 0], across(tiles_end[:]), along(tile_iota[:]), ALU.is_le))
            v.tensor_tensor(per_tile[:, 1], per_tile[:, 0], across(tiles[:]), ALU.mult)
            link(v.tensor_tensor(per_tile[:, 2], across(final[:]), along(tile_iota[:]), ALU.is_equal))
            link(v.tensor_tensor(per_tile[:, 2], per_tile[:, 2], across(back[:]), ALU.mult))
            link(v.tensor_reduce(sums[:], per_tile[:], axis=AX.X, op=ALU.add))
            v.tensor_copy(table_col[:, 0, :], sums[:, 0, :])
            link(v.scalar_tensor_tensor(sums[:, 2, :], sums[:, 0, :], float(REGION), sums[:, 2, :], ALU.mult, ALU.subtract))
            link(v.tensor_tensor(sums[:, 1, :], tile_iota[:], sums[:, 1, :], ALU.subtract))
            v.scalar_tensor_tensor(table_col[:, 1, :], sums[:, 1, :], float(P), sums[:, 2, :], ALU.mult, ALU.add
                                   ).then_inc(S["table"], 1)
            table[0] += 1
            dve.wait_ge(S["tables_turned"], 1)
            v.tensor_copy(expert_tab[:], b6[0:1, 0:TC * P])
            v.tensor_copy(row_tab[:], b7[0:1, 0:TC * P]).then_inc(S["tables_kept"], 2)
            link(v.tensor_tensor(out_shift[:, 0:E], tiles_end[:], tiles[:], ALU.subtract))
            link(v.scalar_tensor_tensor(out_shift[:, 0:E], out_shift[:, 0:E], float(P), region_start[:], ALU.mult, ALU.subtract))
            v.tensor_copy(edge[:, 0, 0:E], region_start[:])
            v.tensor_copy(jump[:, 0, 0:1], out_shift[:, 0:1])
            v.tensor_copy(jump[:, 1, 0:E], back[:])
            v.tensor_scalar_add(edge[:, 1, 0:E], tiles[:], -1.0)
            link(v.tensor_tensor(jump[:, 0, 1:E], out_shift[:, 1:E], out_shift[:, 0:E - 1], ALU.subtract))
            v.tensor_tensor(jump[:, 0, 1:E], jump[:, 0, 1:E], back[:, 0:E - 1], ALU.subtract)
            link(v.scalar_tensor_tensor(edge[:, 1, 0:E], edge[:, 1, 0:E], float(P), region_start[:], ALU.mult, ALU.add))
            slots = slot_all[:].rearrange("p b k -> p (b k)")
            v.tensor_copy(shifted[:], slots).then_inc(S["shift_done"], 1)
            for n in range(2 * E):
                at = (slice(None), n % 2, slice(n // 2, n // 2 + 1))
                dve.wait_ge(S["shift_done"], 2 * n + 1)
                v.tensor_scalar(shift_part[:], slots, edge[at], jump[at], ALU.is_ge, ALU.mult).then_inc(S["shift_done"], 1)
                dve.wait_ge(S["shift_done"], 2 * n + 2)
                v.tensor_tensor(shifted[:], shifted[:], shift_part[:], ALU.add).then_inc(S["shift_done"], 1)
            dve.wait_ge(S["shift_done"], 4 * E + 1)
            v.tensor_copy(out_row[:], shifted[:]).then_inc(S["shift_done"], 1)
            dve.wait_ge(S["gate_exp"], BATCHES)
            all_gates = gate_all[:].rearrange("p b k -> p (b k)")
            v.tensor_scalar_add(all_gates, all_gates, 1.0).then_inc(S["gate_done"], 1)
            dve.wait_ge(S["gate_done"], 1)
            v.reciprocal(all_gates, all_gates).then_inc(S["gate_done"], 1)
            dve.wait_ge(S["gate_done"], 2)
            v.tensor_tensor(gate_sum[:], gate_all[:, :, 0], gate_all[:, :, 1], ALU.add).then_inc(S["gate_done"], 1)
            dve.wait_ge(S["gate_done"], 3)
            v.reciprocal(gate_sum[:], gate_sum[:]).then_inc(S["gate_done"], 1)
            dve.wait_ge(S["gate_done"], 4)
            v.tensor_tensor(gate_all[:], gate_all[:], gate_sum[:].unsqueeze(2).to_broadcast([P, BATCHES, TOP_K]),
                            ALU.mult).then_inc(S["gate_done"], 1)
            dve.wait_ge(S["gate_done"], 5)

            def tile_step(i):
                t, h, d = i.before(1), i.before(2), i.before(3)
                if h.exists():
                    after(dve, S["he_turned"], h)
                    after(dve, S["ye_made"], h.before(2))
                    v.tensor_copy(he_t[h.slot][:], pe_h[h.slot]).then_inc(S["he_kept"], 1)
                if t.exists():
                    after(dve, S["te_done"], t)
                    v.scalar_tensor_tensor(ge[t.slot][:], te[t.slot][:], 1.0, pe_gu[t.slot][:, 0:I],
                                           ALU.add, ALU.mult).then_inc(S["ge_done"], 1)
                    after(dve, S["ge_done"], t)
                    after(dve, S["he_turned"], t.before(2))
                    v.scalar_tensor_tensor(he[t.slot][:], ge[t.slot][:], 0.5, pe_gu[t.slot][:, I:2 * I],
                                           ALU.mult, ALU.mult).then_inc(S["he_done"], 1)
                if d.exists():
                    after(dve, S["ye_made"], d)
                    landed(dve, ye_out, d.before(2))
                    v.tensor_copy(ye[d.slot][:], pe_y[d.slot]).then_inc(S["ye_done"], 1)

            for_all_steps(dve, TILES, 3, tile_step, 4)

            def last_step(i):
                if not i.exists():
                    return
                after(dve, S["total_done"], i.before(2))
                stand(i.slot)
                v.tensor_copy(gates[i.slot][:], gate_all[:, bass.ds(i.number, 1), :].rearrange("p a b -> p (a b)")
                              ).then_inc(S["gates_done"], 1)
                after(dve, S["gates_done"], i)
                landed(dve, first_in, i)
                landed(dve, rest_in, i)
                v.scalar_tensor_tensor(part[i.slot][:], first[i.slot][:], gates[i.slot][:, 0:1], rest[i.slot][:],
                                       ALU.mult, ALU.add).then_inc(S["part_done"], 1)
                after(dve, S["part_done"], i)
                landed(dve, second_in, i)
                landed(dve, total_out, i.before(2))
                v.scalar_tensor_tensor(total[i.slot][:], second[i.slot][:], gates[i.slot][:, 1:2], part[i.slot][:],
                                       ALU.mult, ALU.add).then_inc(S["total_done"], 1)

            for_all_steps(dve, BATCHES, 0, last_step)

        @block.tensor
        def _(pe):
            t = nc.tensor
            t_ = nc.tensor.transpose

            def mm(dst, left, right, first=True, last=True, shared=False):
                return t.matmul(dst, left, right, start=first, stop=last, skip_group_check=shared)

            pe.wait_ge(w_in, 16 * 12)
            pe.wait_ge(setup_p, 4)
            pe.wait_ge(setup_v, 2)
            for c in range(DC):
                mm(b4[:, 0:D], bv_rep[:, c, :], wo_sb[:, c, :], c == 0, False)
            mm(b4[:, 0:D], ones_row[:], wo_b_row[:], False, True)
            mm(b5[:, 0:E], ones_row[:], gate_b_row[:]).then_inc(setup_pe, 1)
            pe.wait_ge(setup_done, 1)
            pe.wait_ge(bias_in, 48)

            def step(i):
                s, o = i.before(1), i.before(2)
                if s.exists():
                    after(pe, S["q_done"], s)
                    after(pe, S["k_lo_done"], s)
                    after(pe, S["probs_done"], s.before(1), 4)
                    for c in range(HC):
                        for k in (k_hi, k_lo):
                            for r in range(4):
                                g = slice(32 * r, 32 * r + 32)
                                m = mm(ps_s[:, r, c * P:(c + 1) * P], q_sb[s.slot][g, c, :], k[s.slot][g, c, :],
                                       c == 0 and k is k_hi, k is k_lo, True)
                                if c == HC - 1 and k is k_lo:
                                    m.then_inc(S["scores_made"], 1)
                if o.exists():
                    after(pe, S["o_done"], o)
                    after_first(pe, (S["base_done"], o.before(1)), (S["v_done"], i.before(1)),
                                (S["max_kept"], s.before(1)))
                    for c in range(DC):
                        m = t.transpose(ps_ot[:, c, :], o_sb[o.slot][:, c * P:(c + 1) * P], ident[:])
                    m.then_inc(S["ot_made"], 1)
                if i.exists():
                    after(pe, S["xn_done"], i)
                    landed(pe, c_in, i)
                    after_first(pe, (S["o_done"], o), (S["rank_done"], o.before(1)),
                                (S["k_lo_done"], i.before(1)))
                    for c in range(DC):
                        t.transpose(ps_xc[:, c, :], xn[i.slot][:, c * P:(c + 1) * P], ident[:])
                    for c in range(DC):
                        m = t.transpose(ps_xc[:, DC + c, :], c_sb[i.slot][:, c * P:(c + 1) * P], ident[:])
                    m.then_inc(S["xc_turned"], 1)
                if o.exists():
                    after(pe, S["ot_kept"], o)
                    after(pe, S["pv_kept"], o)
                    for c in range(DC):
                        m = mm(ps_wo, o_t[o.slot][:, c, :], wo_sb[:, c, :], c == 0, c == DC - 1)
                    m.then_inc(S["wo_made"], 1)

                def project(dst, w, n, x0, done):
                    for g in range(HC):
                        cols = dst[:, g * P:(g + 1) * P]
                        for c in range(DC):
                            mm(cols, w[:, c, g, :], xc_t[i.slot][:, x0 + c, :], c == 0, False)
                        m = mm(cols, bias3[:, n, g * P:(g + 1) * P], ones3[:], False, True)
                    m.then_inc(done, 1)

                if i.exists():
                    after(pe, S["xc_kept"], i)
                    after_first(pe, (S["h_kept"], o.before(1)), (S["q_done"], i.before(1)))
                    project(ps_q, wq_sb, 0, 0, S["q_made"])
                if s.exists():
                    after(pe, S["max_lo_done"], s)
                    after_first(pe, (S["ot_kept"], o), (S["v_done"], i.before(1)))
                    t.transpose(ps_mt, max_parts[s.slot][:].rearrange("p r j -> p (r j)"), ident_bf[:]
                                ).then_inc(S["max_turned"], 1)
                if i.exists():
                    after(pe, S["xc_kept"], i)
                    project(ps_k, wk_sb, 1, DC, S["k_made"])
                if o.exists():
                    after(pe, S["xn2_done"], o)
                    for c in range(DC):
                        m = t.transpose(ps_x2[:, c, :], xn2[o.slot][:, c * P:(c + 1) * P], ident[:])
                    m.then_inc(S["x2_turned"], 1)
                if s.exists():
                    after(pe, S["max_kept"], s)
                    for c in range(HC):
                        for n in range(3):
                            for r in range(4):
                                g = slice(32 * r, 32 * r + 32)
                                left, right = ((k_hi[s.slot][g, c, :], q_sb[s.slot][g, c, :]),
                                               (k_lo[s.slot][g, c, :], q_sb[s.slot][g, c, :]),
                                               (pick[g, c, :], max_t[s.slot][g, :]))[n]
                                m = mm(ps_s[:, r, c * P:(c + 1) * P], left, right, c == 0 and n == 0, n == 2, True)
                                if c == HC - 1 and n == 2:
                                    m.then_inc(S["shifted_made"], 1)
                if o.exists():
                    after(pe, S["x2_kept"], o)
                    after_first(pe, (S["q_done"], i), (S["h_kept"], o.before(1)))
                    for c in range(DC):
                        m = mm(ps_gu, xn2_t[o.slot][:, c, :], gu_sb[:, c, :], c == 0, c == DC - 1)
                    m.then_inc(S["gu_made"], 1)
                if i.exists():
                    after(pe, S["max_kept"], s)
                    for c in range(DC):
                        m = mm(ps_v, xc_t[i.slot][:, DC + c, :], wv_sb[:, c, :], c == 0, c == DC - 1)
                    m.then_inc(S["v_made"], 1)
                if o.exists():
                    after(pe, S["chosen_bf_done"], o)
                    after(pe, S["seen_done"], o.before(1))
                    after_first(pe, (S["k_lo_done"], i), (S["o_done"], o))
                    mm(ps_rank, earlier[:], chosen_bf[o.slot][:], True, False)
                    mm(ps_rank, ones_bf[:], seen[:], False, True).then_inc(S["rank_made"], 1)
                if s.exists():
                    after(pe, S["probs_done"], s, 4)
                    after(pe, S["v_done"], s)
                    after(pe, S["x2_kept"], o)
                    for c in range(HC):
                        for r in range(4):
                            g = slice(32 * r, 32 * r + 32)
                            m = mm(ps_pv[g, c, :], v_sb[s.slot][:, 4 * c + r, :], probs[s.slot][:, r, c, :])
                    m.then_inc(S["pv_made"], 1)
                if o.exists():
                    after(pe, S["h_done"], o)
                    t.transpose(ps_h, h_sb[o.slot][:], ident[:]).then_inc(S["h_turned"], 1)
                    after(pe, S["h_kept"], o)
                    after_first(pe, (S["v_done"], i), (S["max_kept"], s), (S["ot_kept"], o))
                    mm(ps_sd, h_t[o.slot][:], sd_sb[:]).then_inc(S["sd_made"], 1)
                if s.exists():
                    after(pe, S["pv_kept"], s)
                    after_first(pe, (S["rank_done"], o), (S["k_lo_done"], i))
                    for c in range(HC):
                        m = t.transpose(b5[:, c * P:(c + 1) * P], o_un[s.slot][:, c, :], ident[:])
                    m.then_inc(S["o_turned"], 1)

            for_all_steps(pe, BATCHES, 2, step)

            pe.wait_ge(S["seen_done"], BATCHES)
            pe.wait_ge(S["o_done"], BATCHES)
            mm(b5[:, 0:E], ones_bf[:], seen[:]).then_inc(S["counted"], 1)
            pe.wait_ge(S["table"], TABLE_STEPS)
            pe.wait_ge(S["pv_kept"], BATCHES)
            pe.wait_ge(S["h_kept"], BATCHES)
            for n, table in enumerate((b6, b7)):
                for c in range(TC):
                    m = mm(table[0:1, c * P:(c + 1) * P], table_col[:, n, c:c + 1], ident[:])
            m.then_inc(S["tables_turned"], 1)
            pe.wait_ge(w_in2, 32)
            pe.wait_ge(S["tables_kept"], 2)
            pe.wait_ge(S["base_done"], BATCHES)

            def tile_step(i):
                t, h, d = i.before(1), i.before(2), i.before(3)
                if t.exists():
                    e_t = pe.value_load(expert_tab[0:1, bass.ds(t.number, 1)], min_val=0, max_val=E - 1)
                if d.exists():
                    e_d = pe.value_load(expert_tab[0:1, bass.ds(d.number, 1)], min_val=0, max_val=E - 1)
                if i.exists():
                    landed(pe, xe_in, i)
                    after(pe, S["xe_kept"], i.before(2))
                    for c in range(DC):
                        m = t_(pe_xe[i.slot][:, c, :], xe[i.slot4][:, c * P:(c + 1) * P], ident[:])
                    m.then_inc(S["xe_turned"], 1)
                if t.exists():
                    after(pe, S["xe_kept"], t)
                    after(pe, S["he_done"], t.before(2))
                    for c in range(DC):
                        m = mm(pe_gu[t.slot], xe_t[t.slot][:, c, :],
                               eg_sb[:, bass.ds(e_t, 1), c, :].rearrange("p a n -> p (a n)"), c == 0, c == DC - 1)
                    m.then_inc(S["ge_made"], 1)
                if h.exists():
                    after(pe, S["he_done"], h)
                    after(pe, S["he_kept"], h.before(2))
                    t_(pe_h[h.slot], he[h.slot][:], ident[:]).then_inc(S["he_turned"], 1)
                if d.exists():
                    after(pe, S["he_kept"], d)
                    after(pe, S["ye_done"], d.before(2))
                    mm(pe_y[d.slot], he_t[d.slot][:], ed_sb[:, bass.ds(e_d, 1), :].rearrange("p a n -> p (a n)")
                       ).then_inc(S["ye_made"], 1)

            for_all_steps(pe, TILES, 3, tile_step, 4)


def kernel(**inputs):
    import numpy as np
    import concourse.bacc as bacc
    from concourse.bass_utils import run_bass_kernel_spmd

    a = {name: np.asarray(value) for name, value in inputs.items()}
    x = a["x"]
    rows = lambda n: a[n].reshape(1, -1)
    turned = lambda n: np.ascontiguousarray(a[n].T)
    D = x.shape[-1]
    arrays = {
        "x": x.reshape(-1, D), "ctx": a["ctx_1024"].reshape(-1, D),
        "wq_t": turned("L0_xattn_wq_w"), "wq_b": rows("L0_xattn_wq_b"),
        "wk_t": turned("L0_xattn_wk_w"), "wk_b": rows("L0_xattn_wk_b"),
        "wv_t": turned("L0_xattn_wv_w"), "wv_b": np.ascontiguousarray(a["L0_xattn_wv_b"].reshape(-1, P).T),
        "wo_t": turned("L0_xattn_wo_w"), "wo_b": rows("L0_xattn_wo_b"),
        "gate_w": a["L0_ffn_gate_w"], "gate_b": rows("L0_ffn_gate_b"),
        "shared_gu": np.concatenate([a["L0_ffn_shared_wg"], a["L0_ffn_shared_wu"]], axis=1),
        "shared_d": a["L0_ffn_shared_wd"],
        "experts_gu": np.concatenate([a["L0_ffn_experts_wg"], a["L0_ffn_experts_wu"]], axis=2),
        "experts_d": a["L0_ffn_experts_wd"],
    }
    nc = bacc.Bacc("TRN2", target_bir_lowering=False, num_devices=1)
    arrays = {f"in_{name}": np.ascontiguousarray(value) for name, value in arrays.items()}
    operands = [nc.dram_tensor(name, value.shape, fp32, kind="ExternalInput").ap() for name, value in arrays.items()]
    out = nc.dram_tensor("out", (x.shape[0] * x.shape[1], D), fp32, kind="ExternalOutput").ap()
    xattn_moe_kernel(nc, *operands, out)
    result = run_bass_kernel_spmd(nc, [arrays], core_ids=[0])
    return result.results[0]["out"].reshape(x.shape)
```

```python
import concourse.bass as bass
from concourse import mybir
from contextlib import ExitStack

fp32 = mybir.dt.float32
fp16 = mybir.dt.float16
bf16 = mybir.dt.bfloat16
u32 = mybir.dt.uint32
i32 = mybir.dt.int32
ALU = mybir.AluOpType
ACT = mybir.ActivationFunctionType
AX = mybir.AxisListType

P = 128
H, DH = 16, 16
TOP_K = 2
LN_EPS = 1e-5
SIGMOID_ONE = 17.5


class Batch:

    def __init__(self, turn, offset, batches, unroll=2):
        self.turn, self.offset, self.batches, self.unroll = turn, offset, batches, unroll
        self.number = turn * unroll + offset
        self.slot = offset % 2
        self.slot4 = offset % 4

    def before(self, n):
        return Batch(self.turn, self.offset - n, self.batches, self.unroll)

    def exists(self):
        return not isinstance(self.number, int) or 0 <= self.number < self.batches


def after(engine, signal, batch, each=1, nth=None):
    if batch.exists():
        nth = each if nth is None else nth
        engine.wait_ge(signal, batch.turn * (batch.unroll * each) + batch.offset * each + nth)


def landed(engine, signals, batch):
    if batch.exists():
        n = len(signals)
        engine.wait_ge(signals[batch.offset % n],
                       batch.turn * (batch.unroll // n * 16) + (batch.offset // n + 1) * 16)


def after_first(engine, *events):
    for signal, batch in events:
        if batch.exists():
            after(engine, signal, batch)
            return


def for_all_steps(engine, batches, depth, step, unroll=2):
    peeled = 2 * unroll
    for i in range(peeled):
        step(Batch(0, i, batches, unroll))
    with engine.Fori(peeled // unroll, batches // unroll - 1) as turn:
        for u in range(unroll):
            step(Batch(turn, u, batches, unroll))
    for i in range(batches - unroll, batches + depth):
        step(Batch(0, i, batches, unroll))


def xattn_moe_kernel(nc, x, ctx_in, wq_t, wq_b, wk_t, wk_b, wv_t, wv_b, wo_t, wo_b,
                     gate_w, gate_b, shared_gu, shared_d, experts_gu, experts_d, out):
    TOKENS, D = x.shape
    BATCHES = TOKENS // P
    E = gate_w.shape[1]
    I = shared_d.shape[0]
    DC = D // P
    HC = 4
    REGION = TOKENS
    TILES = TOP_K * TOKENS // P + E

    TC = -(-TILES // P)
    TURNS = TILES // 4 + 1
    TABLE_STEPS = 16

    xs_dram = nc.dram_tensor("expert_in", [E * REGION, D], fp32).ap()
    ys_dram = nc.dram_tensor("expert_out", [TILES * P, D], fp32).ap()
    x1_dram = nc.dram_tensor("after_attention", [TOKENS, D], fp32).ap()

    with ExitStack() as stack:
        def sb(name, shape, dt=fp32):
            return stack.enter_context(nc.sbuf_tensor(name, shape, dt))

        def pb(name, shape, dt=fp32):
            return stack.enter_context(nc.psum_tensor(name, shape, dt))

        def sem(name):
            return stack.enter_context(nc.semaphore(name))

        wq_sb = sb("wq_sb", [P, DC, D])
        wk_sb = sb("wk_sb", [P, DC, D])
        wv_sb = sb("wv_sb", [P, DC, D])
        wo_sb = sb("wo_sb", [P, DC, D])
        router_sb = sb("router_sb", [P, DC, E])
        gu_sb = sb("gu_sb", [P, DC, 2 * I])
        sd_sb = sb("sd_sb", [P, D])
        eg_sb = sb("eg_sb", [P, E, DC, 2 * I])
        ed_sb = sb("ed_sb", [P, E, D])
        bias_row = sb("bias_row", [1, 2, D])
        bias_left = sb("bias_left", [1, 2, D])
        bias_parts = sb("bias_parts", [1, 3, 2, D], bf16)
        bias3 = sb("bias3", [3, 2, D], bf16)
        wo_b_row = sb("wo_b_row", [1, D])
        gate_b_row = sb("gate_b_row", [1, E])
        bv_col = sb("bv_col", [P, DC])
        bv_rep = sb("bv_rep", [P, DC, P])
        attn_bias = sb("attn_bias", [P, D])
        gate_bias = sb("gate_bias", [P, E])
        ones_row = sb("ones_row", [1, P])
        ones3 = sb("ones3", [3, P], bf16)
        ones_bf = sb("ones_bf", [P, P], bf16)
        col_iota = sb("col_iota", [P, P])
        row_int = sb("row_int", [P, 1], i32)
        row_int4 = sb("row_int4", [P, 1], i32)
        row_iota = sb("row_iota", [P, 1])
        row_mod4 = sb("row_mod4", [P, 1])
        ident = sb("ident", [P, P])
        ident_bf = sb("ident_bf", [P, P], bf16)
        ident_half = sb("ident_half", [P, P], fp16)
        earlier = sb("earlier", [P, P], bf16)
        pick = sb("pick", [P, HC, P], bf16)
        minus_half = sb("minus_half", [P, 1])
        region_start = sb("region_start", [P, E])
        slot_all = sb("slot_all", [P, BATCHES, TOP_K])
        expert_all = sb("expert_all", [P, BATCHES, TOP_K])
        kept = sb("kept", [P, BATCHES, 4])
        gate_all = kept[:, :, 0:TOP_K]
        seen = sb("seen", [P, E], bf16)
        def two(name, shape, dt=fp32):
            return [sb(f"{name}{n}", shape, dt) for n in range(2)]

        spare_pool, spare_dve = two("spare_pool", [P, 1]), two("spare_dve", [P, 1])
        x_sb = two("x_sb", [P, D])
        c_sb = two("c_sb", [P, D])
        xn = two("xn", [P, D])
        x_res = two("x_res", [P, D])
        stats1, stats2 = two("stats1", [P, 6]), two("stats2", [P, 6])
        mv1, mv2 = two("mv1", [P, 3]), two("mv2", [P, 3])
        ve1, ve2 = two("ve1", [P, 1]), two("ve2", [P, 1])
        xc_t = two("xc_t", [P, 2 * DC, P])
        q_parts = two("q_parts", [P, H, 2, 2, DH], fp16)
        k_parts = two("k_parts", [P, H, 2, 2, DH], fp16)
        q_t = two("q_t", [P, H // 2, P], fp16)
        k_t = two("k_t", [P, H // 2, P], fp16)
        v_sb = two("v_sb", [P, H, 2 * DH])
        neg_max = two("neg_max", [P, 4, HC])
        max_parts = two("max_parts", [P, 4, 32], bf16)
        max_t = two("max_t", [P, P], bf16)
        probs = two("probs", [P, 4, HC, P])
        o_un = two("o_un", [P, HC, P])
        o_rec = two("o_rec", [P, HC, 4])
        o_sb = two("o_sb", [P, D])
        o_t = two("o_t", [P, DC, P])
        x1 = two("x1", [P, D])
        xn2 = [sb(f"xn2_{n}", [P, D]) for n in range(4)]
        xn2_t = two("xn2_t", [P, DC, P])
        key = two("key", [P, E])
        top_v = two("top_v", [P, 8])
        top_i = two("top_i", [P, 8], u32)
        chosen = two("chosen", [P, TOP_K, E])
        chosen_bf = two("chosen_bf", [P, E], bf16)
        rank = two("rank", [P, E])
        rank2 = two("rank2", [P, TOP_K, E])
        slot_int = [sb(f"slot_int{n}", [P, TOP_K], u32) for n in range(4)]

        rows_of = sb("rows_of", [P, E])
        count_int = sb("count_int", [P, E], i32)
        tiles_int = sb("tiles_int", [P, E], i32)
        tiles = sb("tiles", [P, E])
        tiles_end = sb("tiles_end", [P, E])
        final = sb("final", [P, E])
        full = sb("full", [P, E])
        back = sb("back", [P, E])
        edge = sb("edge", [P, 2, E + 1])
        jump = sb("jump", [P, 2, E + 1])
        out_shift = sb("out_shift", [P, E + 1])
        shift_part = sb("shift_part", [P, BATCHES * TOP_K])
        shifted = sb("shifted", [P, BATCHES * TOP_K])
        ones_e = sb("ones_e", [P, E])
        tile_iota = sb("tile_iota", [P, TC])
        last_tile = sb("last_tile", [P, 1])
        per_tile = sb("per_tile", [P, 3, TC, E])
        sums = sb("sums", [P, 3, TC])
        table_col = sb("table_col", [P, 2, TC])
        turn_tab = sb("turn_tab", [1, TURNS], i32)
        packed = [sb(f"packed{n}", [1, TURNS]) for n in range(2)]
        expert_row = sb("expert_row", [1, 4 * TURNS + 8])
        row_tab = sb("row_tab", [1, TC * P], i32)
        zeros = sb("zeros", [P, D])
        gate_sum = sb("gate_sum", [P, BATCHES])
        xe = [sb(f"xe{n}", [P, D]) for n in range(4)]
        xe_t = two("xe_t", [P, DC, P])
        te = two("te", [P, I])
        ge = two("ge", [P, I])
        he = two("he", [P, I])
        he_t = two("he_t", [P, P])
        ye = two("ye", [P, D])
        out_row = sb("out_row", [P, BATCHES * TOP_K], u32)
        gather_row = [sb(f"gather_row{n}", [P, TOP_K], u32) for n in range(4)]
        def four(name, shape):
            return [sb(f"{name}{n}", shape) for n in range(4)]

        first, second = four("first", [P, D]), four("second", [P, D])
        x1_back = two("x1_back", [P, D])
        xn3, xn3_t = two("xn3", [P, D]), two("xn3_t", [P, DC, P])
        both = four("both", [P, D])
        tsh, gsh, hsh, hsh_t = (two(name, [P, I]) for name in ("tsh", "gsh", "hsh", "hsh_t"))
        part, part2 = two("part", [P, D]), two("part2", [P, D])
        total = two("total", [P, D])
        scal = four("scal", [P, 4])

        ps_s = pb("ps_s", [P, 4, 512])
        b4, b5, b6, b7 = (pb(f"b{n}", [P, 512]) for n in (4, 5, 6, 7))
        ps_ot = b4[:, 0:D].rearrange("p (c t) -> p c t", c=DC)
        ps_mt = b4[:, :].bitcast(bf16)[:, 0:P]
        ps_v = b4[:, 0:D]
        ps_qt = b4[:, :].bitcast(fp16).rearrange("p (c t) -> p c t", c=H // 2)
        ps_xc = b5[:, :].rearrange("p (c t) -> p c t", c=2 * DC)
        ps_kt = b5[:, :].bitcast(fp16).rearrange("p (c t) -> p c t", c=H // 2)
        ps_wo = b6[:, 0:D]
        ps_x2 = b6[:, 0:D].rearrange("p (c t) -> p c t", c=DC)
        ps_pv = b6[:, :].rearrange("p (c t) -> p c t", c=HC)
        ps_o = b7[:, :].rearrange("p (c r w) -> p c r w", c=HC, r=4)
        ps_q, ps_k = b7[:, 0:D], b5[:, 0:D]
        ps_router = b7[:, 0:E]
        ps_rank = b7[:, E:2 * E]

        pe_xe = [ps_s[:, n, 0:D].rearrange("p (c t) -> p c t", c=DC) for n in range(2)]
        pe_gu = [ps_s[:, 2 + n, 0:2 * I] for n in range(2)]
        pe_h = [b4[:, 0:P], b5[:, 0:P]]
        pe_y = [b6[:, 0:D], b7[:, 0:D]]

        w_in, w_in2 = sem("w_in"), sem("w_in2")
        consts, bias_split, bias_in, setup_v, setup_pe, setup_done = (
            sem(n) for n in ("consts", "bias_split", "bias_in", "setup_v", "setup_pe", "setup_done"))
        setup_p = sem("setup_p")
        zeroed = sem("zeroed")
        x_in = [sem(f"x_in{n}") for n in range(2)]
        x1_out = [sem(f"x1_out{n}") for n in range(2)]
        c_in = [sem(f"c_in{n}") for n in range(2)]
        names = """stats1_done mv1_done ve1_done rstd1_done xn_done x_res_done
            xc_turned xc_kept q_made q_hi_done q_lo_done k_made k_hi_done k_lo_done
            q_turned q_kept k_turned k_kept v_made v_done
            scores_made max_taken max_hi_done max_lo_done max_turned max_kept shifted_made
            probs_done pv_made pv_kept o_turned rec_done o_done
            ot_made ot_kept wo_made x1_done stats2_done mv2_done ve2_done rstd2_done xn2_done
            x2_turned x2_kept logits_made biased_done key_done topv_done topi_done expert_done
            chosen_done chosen_bf_done gate_exp norm_kept rank_made seen_done
            rank_done rank2_done slotf_done slot_done
            sent counted packed_done table tables_turned tables_kept shift_done gate_done
            xe_turned xe_kept ge_made te_done ge_done he_done he_turned he_kept ye_made ye_done
            scal_done xn3_done both_done xn3_turned xn3_kept gsh_made tsh_done gsh_done hsh_done
            hsh_turned hsh_kept shared_made gather_row_done gather_stood part_done part2_done
            total_done""".split()
        S = {n: sem(n) for n in names}
        xe_in = [sem(f"xe_in{n}") for n in range(4)]
        ye_out, x1_in, total_out = (
            [sem(f"{name}{n}") for n in range(2)] for name in ("ye_out", "x1_in", "total_out"))
        first_in, second_in = (
            [sem(f"{name}{n}") for n in range(4)] for name in ("first_in", "second_in"))

        block = stack.enter_context(nc.Block())

        def rows(dram, batch):
            return dram[bass.ds(batch.number * P, P), :]

        def read_registers(engine, numbers, largest):
            _, values = nc.values_load_multi_w_load_instructions(
                numbers, engines=[engine], min_val=0, max_val=largest)
            return list(values)

        @block.sync
        def _(sp):
            chunked = lambda w: w.rearrange("(c p) n -> p c n", p=P)
            for dst, src in ((wq_sb[:], chunked(wq_t)), (wk_sb[:], chunked(wk_t)),
                             (bias_row[:, 0, :], wq_b), (bias_row[:, 1, :], wk_b),
                             (wv_sb[:], chunked(wv_t)), (wo_sb[:], chunked(wo_t)),
                             (bv_col[:], wv_b), (wo_b_row[:], wo_b), (gate_b_row[:], gate_b),
                             (router_sb[:], chunked(gate_w)),
                             (gu_sb[:], chunked(shared_gu)), (sd_sb[:], shared_d)):
                sp.dma_start(dst, src).then_inc(w_in, 16)
            for b in range(2):
                sp.dma_start(x_sb[b][:], x[b * P:(b + 1) * P, :]).then_inc(x_in[b], 16)
            sp.dma_start(c_sb[0][:], ctx_in[0:P, :]).then_inc(c_in[0], 16)
            sp.wait_ge(consts, 2)
            for e in range(E):
                sp.dma_start(xs_dram[e * REGION:e * REGION + P, :], zeros[:]).then_inc(zeroed, 16)
            sp.wait_ge(bias_split, 5)
            for n in range(3):
                sp.dma_start(bias3[n:n + 1, :, :], bias_parts[:, n, :, :]).then_inc(bias_in, 16)
            sp.dma_start(eg_sb[:], experts_gu.rearrange("e (c p) n -> p e c n", p=P)).then_inc(w_in2, 16)
            sp.dma_start(ed_sb[:], experts_d.rearrange("e p n -> p e n")).then_inc(w_in2, 16)

            def step(i):
                b = i.before(-1)
                if b.exists():
                    after(sp, S["xc_turned"], b.before(2))
                    sp.dma_start(c_sb[b.slot][:], rows(ctx_in, b)).then_inc(c_in[b.slot], 16)
                b = i.before(2)
                if b.exists():
                    after(sp, S["x1_done"], b)
                    sp.dma_start(rows(x1_dram, b), x1[b.slot][:]).then_inc(x1_out[b.slot], 16)
                b = i.before(-2)
                if b.exists():
                    after(sp, S["x_res_done"], i)
                    after(sp, S["xn_done"], i)
                    sp.dma_start(x_sb[b.slot][:], rows(x, b)).then_inc(x_in[b.slot], 16)

            for_all_steps(sp, BATCHES, 2, step, 4)

            for n in range(2):
                sp.wait_ge(x1_out[n], BATCHES // 2 * 16)
            sp.wait_ge(S["sent"], 32 * BATCHES)
            sp.wait_ge(S["tables_kept"], 2)

            first_rows = []

            def tile_step(i):
                if i.slot4 == 0:
                    first_rows[:] = read_registers(mybir.EngineType.SP, row_tab[0:1, bass.ds(i.number, 4)],
                                                   E * REGION - P)
                after(sp, S["xe_turned"], i.before(4))
                sp.dma_start(xe[i.slot4][:], xs_dram[bass.ds(first_rows[i.slot4], P), :]
                             ).then_inc(xe_in[i.slot4], 16)

            for_all_steps(sp, TILES, 0, tile_step, 4)

            def last_step(i):
                if i.exists():
                    after(sp, S["both_done"], i.before(2))
                    sp.dma_start(x1_back[i.slot][:], rows(x1_dram, i)).then_inc(x1_in[i.slot], 16)
                o = i.before(5)
                if o.exists():
                    after(sp, S["total_done"], o)
                    sp.dma_start(rows(out, o), total[o.slot][:]).then_inc(total_out[o.slot], 16)

            for_all_steps(sp, BATCHES, 5, last_step, 4)
            for n in range(2):
                sp.wait_ge(total_out[n], BATCHES // 2 * 16)

        @block.gpsimd
        def _(pool):
            g = nc.gpsimd

            def stand(b, signal):
                after(pool, signal, b.before(2))
                g.tensor_tensor(spare_pool[b.slot][:], minus_half[:], minus_half[:],
                                ALU.add).then_inc(signal, 1)

            g.iota(col_iota[:], pattern=[[1, P]], base=0, channel_multiplier=0,
                   allow_small_or_imprecise_dtypes=True)
            g.iota(row_int[:], pattern=[[0, 1]], base=0, channel_multiplier=1)
            g.iota(region_start[:], pattern=[[REGION, E]], base=0, channel_multiplier=0,
                   allow_small_or_imprecise_dtypes=True)
            g.memset(minus_half[:], -0.5)
            g.memset(ones_row[:], 1.0)
            g.memset(ones3[:], 1.0)
            g.memset(ones_bf[:], 1.0)
            g.memset(seen[:], 0.0)
            for n in range(2):
                g.memset(v_sb[n][:, :, DH:DH + 1], 1.0)
                g.memset(v_sb[n][:, :, DH + 1:], 0.0)
                g.memset(max_parts[n][:], 0.0)
            g.memset(probs[0][:, 0, 0, 0:1], 0.0).then_inc(consts, 1)
            g.iota(tile_iota[:], pattern=[[P, TC]], base=0, channel_multiplier=1,
                   allow_small_or_imprecise_dtypes=True)
            g.memset(zeros[:], 0.0)
            g.memset(expert_row[:], 0.0)
            g.memset(ones_e[:], 1.0).then_inc(consts, 1)
            pool.wait_ge(consts, 2)

            def norm_pow(b, source, target, ready, free, done):
                after(pool, ready, b)
                after(pool, free, b.before(2))
                g.tensor_tensor(target[b.slot][:, 2:3], source[b.slot][:], minus_half[:],
                                ALU.pow).then_inc(done, 1)

            def scatter_free(b, k):
                if k == 0 and isinstance(b.number, int) and b.number == 0:
                    pool.wait_ge(zeroed, 16 * E)
                after(pool, S["slot_done"], b)
                if k:
                    after(pool, S["sent"], b, 32, 16)
                else:
                    after(pool, S["sent"], b.before(1), 32)

            def scatter(b, k):
                g.indirect_dma_start(
                    xs_dram[:, :], bass.IndirectOffsetOnAxis(ap=slot_int[b.slot4][:, k:k + 1], axis=0),
                    xn2[b.slot4][:], None).then_inc(S["sent"], 16)

            norm_pow(Batch(0, 0, BATCHES), ve1, mv1, S["ve1_done"], S["xn_done"], S["rstd1_done"])

            def step(i):
                o, p, n = i.before(2), i.before(3), i.before(-1)
                b = p.before(1)
                if b.exists():
                    scatter_free(b, 1)
                if p.exists():
                    after(pool, S["rank_made"], p)
                    after(pool, S["seen_done"], p.before(1))
                    g.tensor_tensor(seen[:], seen[:], chosen_bf[p.slot][:],
                                    ALU.add).then_inc(S["seen_done"], 1)
                if b.exists():
                    scatter(b, 1)
                if p.exists():
                    scatter_free(p, 0)
                if o.exists():
                    norm_pow(o, ve2, mv2, S["ve2_done"], S["norm_kept"], S["rstd2_done"])
                if p.exists():
                    scatter(p, 0)
                if n.exists():
                    norm_pow(n, ve1, mv1, S["ve1_done"], S["xn_done"], S["rstd1_done"])
                if i.exists():
                    if isinstance(i.number, int) and i.number == 0:
                        pool.wait_ge(setup_done, 1)
                    landed(pool, x_in, i)
                    after(pool, S["x1_done"], i.before(2))
                    g.tensor_tensor(x_res[i.slot][:], x_sb[i.slot][:], attn_bias[:],
                                    ALU.add).then_inc(S["x_res_done"], 1)

            for_all_steps(pool, BATCHES, 3, step, 4)
            scatter_free(Batch(0, BATCHES - 1, BATCHES), 1)
            scatter(Batch(0, BATCHES - 1, BATCHES), 1)

            pool.wait_ge(S["shift_done"], 4 * E + 2)
            for n in range(2):
                pool.wait_ge(ye_out[n], TILES // 2 * 16)

            def last_step(i):
                if not i.exists():
                    return
                landed(pool, first_in, i.before(4))
                landed(pool, second_in, i.before(4))
                g.tensor_copy(gather_row[i.slot4][:], out_row[:, bass.ds(i.number * TOP_K, TOP_K)]
                              ).then_inc(S["gather_row_done"], 1)
                after(pool, S["gather_row_done"], i)
                after(pool, S["part2_done"], i.before(4))
                stand(i, S["gather_stood"])
                for k, (dst, signal) in enumerate(((first, first_in), (second, second_in))):
                    g.indirect_dma_start(dst[i.slot4][:], None, ys_dram[:, :], bass.IndirectOffsetOnAxis(
                        ap=gather_row[i.slot4][:, k:k + 1], axis=0)).then_inc(signal[i.slot4], 16)

            for_all_steps(pool, BATCHES, 0, last_step, 4)

        @block.scalar
        def _(act):
            a = nc.scalar
            def copy(dst, src):
                return a.activation(dst, src, ACT.Copy)

            act.wait_ge(setup_v, 1)

            def step(i):
                s, o = i.before(1), i.before(2)

                def exps(r):
                    after(act, S["shifted_made"], s, 4, r + 1)
                    after(act, S["pv_made"], s.before(2))
                    a.activation(probs[s.slot][:, r, :, :], ps_s[:, r, :].rearrange("p (c t) -> p c t", c=HC),
                                 ACT.Exp, scale=DH ** -0.5).then_inc(S["probs_done"], 1)

                def twice(ps):
                    return ps.rearrange("p (h w) -> p h w", h=H).unsqueeze(2).to_broadcast([P, H, 2, DH])

                if i.exists():
                    after(act, S["xc_turned"], i)
                    after(act, S["v_made"], i.before(2))
                    copy(xc_t[i.slot][:], ps_xc).then_inc(S["xc_kept"], 1)
                if s.exists():
                    after(act, S["v_made"], s)
                    after(act, S["pv_made"], s.before(2))
                    copy(v_sb[s.slot][:, :, 0:DH], ps_v.rearrange("p (h w) -> p h w", h=H)
                         ).then_inc(S["v_done"], 1)
                if i.exists():
                    after(act, S["q_made"], i)
                    after(act, S["q_turned"], i.before(2))
                    copy(q_parts[i.slot][:, :, :, 0, :], twice(ps_q)).then_inc(S["q_hi_done"], 1)
                if o.exists():
                    after(act, S["ot_made"], o)
                    after(act, S["wo_made"], o.before(2))
                    copy(o_t[o.slot][:], ps_ot).then_inc(S["ot_kept"], 1)
                if s.exists():
                    after(act, S["max_turned"], s)
                    after(act, S["shifted_made"], s.before(2), 4)
                    copy(max_t[s.slot][:], ps_mt).then_inc(S["max_kept"], 1)
                if i.exists():
                    after(act, S["k_made"], i)
                    after(act, S["k_turned"], i.before(2))
                    copy(k_parts[i.slot][:, :, 0, :, :], twice(ps_k)).then_inc(S["k_hi_done"], 1)
                if s.exists():
                    exps(0)
                    exps(1)
                    exps(2)
                    exps(3)
                if o.exists():
                    after(act, S["x2_turned"], o)
                    after(act, S["logits_made"], o.before(2))
                    copy(xn2_t[o.slot][:], ps_x2).then_inc(S["x2_kept"], 1)
                if i.exists():
                    for turned, ps, dst, ready, kept_now in ((S["q_turned"], ps_qt, q_t, "q", S["q_kept"]),
                                                            (S["k_turned"], ps_kt, k_t, "k", S["k_kept"])):
                        after(act, turned, i)
                        after(act, S["shifted_made"], i.before(2), 4)
                        copy(dst[i.slot][:], ps).then_inc(kept_now, 1)
                if o.exists():
                    after(act, S["rstd2_done"], o)
                    a.activation(kept[:, bass.ds(o.number, 1), 2:4],
                                 mv2[o.slot][:, 0:3:2].rearrange("p (a b) -> p a b", a=1),
                                 ACT.Copy).then_inc(S["norm_kept"], 1)
                    after(act, S["topv_done"], o)
                    a.activation(kept[:, bass.ds(o.number, 1), 0:2], top_v[o.slot][:, 0:TOP_K].rearrange("p (a b) -> p a b", a=1),
                                 ACT.Exp, scale=-1.0).then_inc(S["gate_exp"], 1)
                if s.exists():
                    after(act, S["pv_made"], s)
                    after(act, S["o_turned"], s.before(2))
                    copy(o_un[s.slot][:], ps_pv).then_inc(S["pv_kept"], 1)

            for_all_steps(act, BATCHES, 2, step, 4)

            def tile_step(i):
                t, y = i.before(1), i.before(4)
                if i.exists():
                    after(act, S["xe_turned"], i)
                    after(act, S["ge_made"], i.before(2))
                    copy(xe_t[i.slot][:], pe_xe[i.slot]).then_inc(S["xe_kept"], 1)
                if t.exists():
                    after(act, S["ge_made"], t)
                    after(act, S["ge_done"], t.before(2))
                    a.activation(te[t.slot][:], pe_gu[t.slot][:, 0:I], ACT.Tanh, scale=0.5
                                 ).then_inc(S["te_done"], 1)
                if y.exists():
                    after(act, S["ye_done"], y)
                    act.dma_start(rows(ys_dram, y), ye[y.slot][:]).then_inc(ye_out[y.slot], 16)

            for_all_steps(act, TILES, 4, tile_step, 4)

            def last_step(i):
                t, h = i.before(1), i.before(3)
                if h.exists():
                    after(act, S["hsh_turned"], h)
                    after(act, S["shared_made"], h.before(2))
                    copy(hsh_t[h.slot][:], pe_h[h.slot]).then_inc(S["hsh_kept"], 1)
                if t.exists():
                    after(act, S["gsh_made"], t)
                    after(act, S["gsh_done"], t.before(2))
                    a.activation(tsh[t.slot][:], pe_gu[t.slot][:, 0:I], ACT.Tanh, scale=0.5
                                 ).then_inc(S["tsh_done"], 1)
                if i.exists():
                    after(act, S["xn3_turned"], i)
                    after(act, S["gsh_made"], i.before(2))
                    copy(xn3_t[i.slot][:], pe_xe[i.slot]).then_inc(S["xn3_kept"], 1)

            for_all_steps(act, BATCHES, 3, last_step, 4)

        @block.vector
        def _(dve):
            v = nc.vector

            def stand(slot):
                v.memset(spare_dve[slot][:], 0.0)


            dve.wait_ge(consts, 1)
            v.tensor_copy(row_iota[:], row_int[:])
            v.tensor_scalar(row_int4[:], row_int[:], 3, None, ALU.bitwise_and).then_inc(setup_v, 1)
            dve.wait_ge(setup_v, 1)
            v.tensor_copy(row_mod4[:], row_int4[:])
            v.tensor_scalar(ident[:], col_iota[:], row_iota[:, 0:1], None, ALU.is_equal)
            v.tensor_scalar(ident_bf[:], col_iota[:], row_iota[:, 0:1], None, ALU.is_equal)
            v.tensor_scalar(ident_half[:], col_iota[:], row_iota[:, 0:1], None, ALU.is_equal)
            v.tensor_scalar(earlier[:], col_iota[:], row_iota[:, 0:1], None,
                            ALU.is_gt).then_inc(setup_v, 1)
            dve.wait_ge(setup_v, 2)
            for c in range(HC):
                v.tensor_scalar(pick[:, c, :], row_mod4[:, 0:1].to_broadcast([P, P]), float(c),
                                None, ALU.is_equal)
            dve.wait_ge(w_in, 16 * 12)
            v.tensor_copy(bv_rep[:], bv_col[:, :].unsqueeze(2).to_broadcast([P, DC, P])).then_inc(setup_p, 1)
            v.tensor_copy(bias_parts[:, 0], bias_row[:]).then_inc(bias_split, 1)
            dve.wait_ge(bias_split, 1)
            v.tensor_tensor(bias_left[:], bias_row[:], bias_parts[:, 0], ALU.subtract).then_inc(bias_split, 1)
            dve.wait_ge(bias_split, 2)
            v.tensor_copy(bias_parts[:, 1], bias_left[:]).then_inc(bias_split, 1)
            dve.wait_ge(bias_split, 3)
            v.tensor_tensor(bias_row[:], bias_left[:], bias_parts[:, 1], ALU.subtract).then_inc(bias_split, 1)
            dve.wait_ge(bias_split, 4)
            v.tensor_copy(bias_parts[:, 2], bias_row[:]).then_inc(bias_split, 1)
            dve.wait_ge(setup_pe, 1)
            v.tensor_copy(attn_bias[:], b4[:, 0:D])
            v.tensor_copy(gate_bias[:], b5[:, 0:E]).then_inc(setup_done, 1)

            def stats_of(b, source, ready, stats, mv, ve, sems, free_mv, free_ve):
                if isinstance(ready, list):
                    landed(dve, ready, b)
                else:
                    after(dve, ready, b)
                v.bn_stats(stats[b.slot][:], source[b.slot][:]).then_inc(S[sems[0]], 1)
                after(dve, S[sems[0]], b)
                after(dve, free_mv, b.before(2))
                stand(b.slot)
                v.bn_aggr(mv[b.slot][:, 0:2], stats[b.slot][:]).then_inc(S[sems[1]], 1)
                after(dve, S[sems[1]], b)
                after(dve, free_ve, b.before(2))
                v.tensor_scalar_add(ve[b.slot][:], mv[b.slot][:, 1:2], LN_EPS).then_inc(S[sems[2]], 1)

            def normalise(b, source, target, mv, ready, done):
                after(dve, ready, b)
                v.tensor_scalar(target[b.slot if len(target) == 2 else b.slot4][:], source[b.slot][:], mv[b.slot][:, 0:1],
                                mv[b.slot][:, 2:3], ALU.subtract, ALU.mult).then_inc(done, 1)

            def stats_x(b):
                stats_of(b, x_sb, x_in, stats1, mv1, ve1, ("stats1_done", "mv1_done", "ve1_done"),
                         S["xn_done"], S["rstd1_done"])

            def normalise_x(b):
                after(dve, S["xc_turned"], b.before(2))
                normalise(b, x_sb, xn, mv1, S["rstd1_done"], S["xn_done"])

            stats_x(Batch(0, 0, BATCHES))
            normalise_x(Batch(0, 0, BATCHES))

            def step(i):
                s, o, p, n = i.before(1), i.before(2), i.before(3), i.before(-1)

                def maxima(r):
                    after(dve, S["scores_made"], s, 4, r + 1)
                    after(dve, S["max_lo_done"], s.before(2))
                    v.tensor_reduce(neg_max[s.slot][:, r, :], ps_s[:, r, :].rearrange("p (c t) -> p c t", c=HC),
                                    axis=AX.X, op=ALU.max, negate=True).then_inc(S["max_taken"], 1)

                def rest_of(ps, parts, low, hi_done, turned, lo_done):
                    after(dve, hi_done, i)
                    after(dve, turned, i.before(2))
                    hi, lo = ((parts[i.slot][:, :, :, 0, :], parts[i.slot][:, :, :, 1, :]) if low == "inner" else
                              (parts[i.slot][:, :, 0, :, :], parts[i.slot][:, :, 1, :, :]))
                    v.tensor_tensor(lo, ps.rearrange("p (h w) -> p h w", h=H).unsqueeze(2).to_broadcast([P, H, 2, DH]),
                                    hi, ALU.subtract).then_inc(lo_done, 1)

                if p.exists():
                    after(dve, S["rank_made"], p)
                    v.tensor_tensor(rank[p.slot][:], ps_rank, region_start[:], ALU.add).then_inc(S["rank_done"], 1)
                if s.exists():
                    maxima(0)
                    maxima(1)
                if o.exists():
                    after(dve, S["o_turned"], o)
                    after(dve, S["o_done"], o.before(2))
                    v.reciprocal(o_rec[o.slot][:], ps_o[:, :, :, DH]).then_inc(S["rec_done"], 1)
                    after(dve, S["rec_done"], o)
                    after(dve, S["ot_made"], o.before(2))
                    v.tensor_tensor(o_sb[o.slot][:].rearrange("p (c r w) -> p c r w", c=HC, r=4),
                                    ps_o[:, :, :, 0:DH], o_rec[o.slot][:].unsqueeze(3).to_broadcast([P, HC, 4, DH]),
                                    ALU.mult).then_inc(S["o_done"], 1)
                if s.exists():
                    maxima(2)
                    maxima(3)
                    after(dve, S["max_taken"], s, 4)
                    after(dve, S["max_turned"], s.before(2))
                    v.tensor_copy(max_parts[s.slot][:, :, 0:HC], neg_max[s.slot][:]).then_inc(S["max_hi_done"], 1)
                    after(dve, S["max_hi_done"], s)
                    v.tensor_tensor(max_parts[s.slot][:, :, HC:2 * HC], neg_max[s.slot][:],
                                    max_parts[s.slot][:, :, 0:HC], ALU.subtract).then_inc(S["max_lo_done"], 1)
                if p.exists():
                    after(dve, S["rank_done"], p)
                    v.tensor_tensor(rank2[p.slot][:], chosen[p.slot][:],
                                    rank[p.slot][:, :].unsqueeze(1).to_broadcast([P, TOP_K, E]),
                                    ALU.mult).then_inc(S["rank2_done"], 1)
                    after(dve, S["rank2_done"], p)
                    v.tensor_reduce(slot_all[:, bass.ds(p.number, 1), :].rearrange("p a b -> p (a b)"), rank2[p.slot][:],
                                    axis=AX.X, op=ALU.add).then_inc(S["slotf_done"], 1)
                    after(dve, S["slotf_done"], p)
                    after(dve, S["sent"], p.before(4), 32)
                    stand(p.slot)
                    v.tensor_copy(slot_int[p.slot4][:], slot_all[:, bass.ds(p.number, 1), :].rearrange("p a b -> p (a b)")
                                  ).then_inc(S["slot_done"], 1)
                if i.exists():
                    rest_of(ps_q, q_parts, "inner", S["q_hi_done"], S["q_turned"], S["q_lo_done"])
                if o.exists():
                    after(dve, S["wo_made"], o)
                    after(dve, S["x_res_done"], o)
                    after(dve, S["xn2_done"], o.before(2))
                    landed(dve, x1_out, o.before(2))
                    v.tensor_tensor(x1[o.slot][:], ps_wo, x_res[o.slot][:], ALU.add).then_inc(S["x1_done"], 1)
                    after(dve, S["norm_kept"], o.before(2))
                    stats_of(o, x1, S["x1_done"], stats2, mv2, ve2,
                             ("stats2_done", "mv2_done", "ve2_done"), S["xn2_done"], S["rstd2_done"])
                if i.exists():
                    rest_of(ps_k, k_parts, "outer", S["k_hi_done"], S["k_turned"], S["k_lo_done"])
                if o.exists():
                    after(dve, S["sent"], o.before(4), 32)
                    normalise(o, x1, xn2, mv2, S["rstd2_done"], S["xn2_done"])
                if n.exists():
                    stats_x(n)
                if o.exists():
                    after(dve, S["logits_made"], o)
                    after(dve, S["key_done"], o.before(1))
                    v.tensor_tensor(key[o.slot][:], ps_router, gate_bias[:], ALU.add).then_inc(S["biased_done"], 1)
                    after(dve, S["biased_done"], o)
                    v.tensor_scalar_min(key[o.slot][:], key[o.slot][:], SIGMOID_ONE).then_inc(S["key_done"], 1)
                    after(dve, S["key_done"], o)
                    after(dve, S["gate_exp"], o.before(2))
                    stand(o.slot)
                    v.max(top_v[o.slot][:], key[o.slot][:]).then_inc(S["topv_done"], 1)
                    after(dve, S["topv_done"], o)
                    stand(o.slot)
                    v.max_index(top_i[o.slot][:], top_v[o.slot][:], key[o.slot][:]).then_inc(S["topi_done"], 1)
                    after(dve, S["topi_done"], o)
                    stand(o.slot)
                    v.tensor_copy(expert_all[:, bass.ds(o.number, 1), :].rearrange("p a b -> p (a b)"),
                                  top_i[o.slot][:, 0:TOP_K]).then_inc(S["expert_done"], 1)
                    after(dve, S["expert_done"], o)
                    v.tensor_tensor(chosen[o.slot][:], col_iota[:, 0:E].unsqueeze(1).to_broadcast([P, TOP_K, E]),
                                    expert_all[:, bass.ds(o.number, 1), :].rearrange("p a b -> p (a b)").unsqueeze(2).to_broadcast([P, TOP_K, E]),
                                    ALU.is_equal).then_inc(S["chosen_done"], 1)
                    after(dve, S["chosen_done"], o)
                    after(dve, S["seen_done"], o.before(2))
                    v.tensor_tensor(chosen_bf[o.slot][:], chosen[o.slot][:, 0, :], chosen[o.slot][:, 1, :],
                                    ALU.add).then_inc(S["chosen_bf_done"], 1)
                if n.exists():
                    normalise_x(n)
            for_all_steps(dve, BATCHES, 3, step, 4)

            def link(instruction):
                instruction.then_inc(S["table"], 1)
                table[0] += 1
                dve.wait_ge(S["table"], table[0])

            table = [0]
            dve.wait_ge(consts, 2)
            dve.wait_ge(S["counted"], 1)
            across = lambda t: t.unsqueeze(1).to_broadcast([P, TC, E])
            along = lambda t: t.unsqueeze(2).to_broadcast([P, TC, E])
            link(v.tensor_copy(rows_of[:], b5[:, 0:E]))
            link(v.tensor_scalar_add(count_int[:], rows_of[:], float(P - 1)))
            link(v.tensor_scalar(tiles_int[:], count_int[:], P.bit_length() - 1, None, ALU.logical_shift_right))
            link(v.tensor_copy(tiles[:], tiles_int[:]))
            link(v.tensor_tensor_scan(tiles_end[:], ones_e[:], tiles[:], 0.0, ALU.mult, ALU.add))
            v.tensor_scalar_add(final[:], tiles_end[:], -1.0)
            v.tensor_scalar(full[:], rows_of[:], float(P), None, ALU.is_ge)
            link(v.tensor_scalar_add(last_tile[:], tiles_end[:, E - 1:E], -1.0))
            link(v.scalar_tensor_tensor(back[:], tiles[:], float(P), rows_of[:], ALU.mult, ALU.subtract))
            link(v.tensor_tensor(back[:], back[:], full[:], ALU.mult))
            link(v.tensor_scalar(tile_iota[:], tile_iota[:], last_tile[:, 0:1], None, ALU.min))
            link(v.tensor_tensor(per_tile[:, 0], across(tiles_end[:]), along(tile_iota[:]), ALU.is_le))
            v.tensor_tensor(per_tile[:, 1], per_tile[:, 0], across(tiles[:]), ALU.mult)
            link(v.tensor_tensor(per_tile[:, 2], across(final[:]), along(tile_iota[:]), ALU.is_equal))
            link(v.tensor_tensor(per_tile[:, 2], per_tile[:, 2], across(back[:]), ALU.mult))
            link(v.tensor_reduce(sums[:], per_tile[:], axis=AX.X, op=ALU.add))
            v.tensor_copy(table_col[:, 0, :], sums[:, 0, :])
            link(v.scalar_tensor_tensor(sums[:, 2, :], sums[:, 0, :], float(REGION), sums[:, 2, :], ALU.mult, ALU.subtract))
            link(v.tensor_tensor(sums[:, 1, :], tile_iota[:], sums[:, 1, :], ALU.subtract))
            v.scalar_tensor_tensor(table_col[:, 1, :], sums[:, 1, :], float(P), sums[:, 2, :], ALU.mult, ALU.add
                                   ).then_inc(S["table"], 1)
            table[0] += 1
            dve.wait_ge(S["tables_turned"], 1)
            v.tensor_copy(row_tab[:], b7[0:1, 0:TC * P]).then_inc(S["tables_kept"], 1)
            v.tensor_copy(expert_row[:, 3:3 + TILES], b6[0:1, 0:TILES]).then_inc(S["packed_done"], 1)
            dve.wait_ge(S["packed_done"], 1)
            digit = lambda n: expert_row[:, n:n + 4 * TURNS].rearrange("p (t f) -> p t f", f=4)[:, :, 0]
            v.tensor_copy(packed[1][:], digit(5)).then_inc(S["packed_done"], 1)
            for n in range(4, -1, -1):
                dve.wait_ge(S["packed_done"], 6 - n)
                v.scalar_tensor_tensor(packed[n % 2][:], packed[(n + 1) % 2][:], 16.0, digit(n),
                                       ALU.mult, ALU.add).then_inc(S["packed_done"], 1)
            dve.wait_ge(S["packed_done"], 7)
            v.tensor_copy(turn_tab[:], packed[0][:]).then_inc(S["tables_kept"], 1)
            link(v.tensor_tensor(out_shift[:, 0:E], tiles_end[:], tiles[:], ALU.subtract))
            link(v.scalar_tensor_tensor(out_shift[:, 0:E], out_shift[:, 0:E], float(P), region_start[:], ALU.mult, ALU.subtract))
            v.tensor_copy(edge[:, 0, 0:E], region_start[:])
            v.tensor_copy(jump[:, 0, 0:1], out_shift[:, 0:1])
            v.tensor_copy(jump[:, 1, 0:E], back[:])
            v.tensor_scalar_add(edge[:, 1, 0:E], tiles[:], -1.0)
            link(v.tensor_tensor(jump[:, 0, 1:E], out_shift[:, 1:E], out_shift[:, 0:E - 1], ALU.subtract))
            v.tensor_tensor(jump[:, 0, 1:E], jump[:, 0, 1:E], back[:, 0:E - 1], ALU.subtract)
            link(v.scalar_tensor_tensor(edge[:, 1, 0:E], edge[:, 1, 0:E], float(P), region_start[:], ALU.mult, ALU.add))
            slots = slot_all[:].rearrange("p b k -> p (b k)")
            v.tensor_copy(shifted[:], slots).then_inc(S["shift_done"], 1)
            for n in range(2 * E):
                at = (slice(None), n % 2, slice(n // 2, n // 2 + 1))
                dve.wait_ge(S["shift_done"], 2 * n + 1)
                v.tensor_scalar(shift_part[:], slots, edge[at], jump[at], ALU.is_ge, ALU.mult).then_inc(S["shift_done"], 1)
                dve.wait_ge(S["shift_done"], 2 * n + 2)
                v.tensor_tensor(shifted[:], shifted[:], shift_part[:], ALU.add).then_inc(S["shift_done"], 1)
            dve.wait_ge(S["shift_done"], 4 * E + 1)
            v.tensor_copy(out_row[:], shifted[:]).then_inc(S["shift_done"], 1)
            dve.wait_ge(S["gate_exp"], BATCHES)
            v.tensor_scalar_add(gate_all, gate_all, 1.0).then_inc(S["gate_done"], 1)
            dve.wait_ge(S["gate_done"], 1)
            v.reciprocal(gate_all, gate_all).then_inc(S["gate_done"], 1)
            dve.wait_ge(S["gate_done"], 2)
            v.tensor_tensor(gate_sum[:], gate_all[:, :, 0], gate_all[:, :, 1], ALU.add).then_inc(S["gate_done"], 1)
            dve.wait_ge(S["gate_done"], 3)
            v.reciprocal(gate_sum[:], gate_sum[:]).then_inc(S["gate_done"], 1)
            dve.wait_ge(S["gate_done"], 4)
            v.tensor_tensor(gate_all, gate_all, gate_sum[:].unsqueeze(2).to_broadcast([P, BATCHES, TOP_K]),
                            ALU.mult).then_inc(S["gate_done"], 1)
            dve.wait_ge(S["gate_done"], 5)

            def tile_step(i):
                t, h, d = i.before(1), i.before(2), i.before(3)
                if h.exists():
                    after(dve, S["he_turned"], h)
                    after(dve, S["ye_made"], h.before(2))
                    v.tensor_copy(he_t[h.slot][:], pe_h[h.slot]).then_inc(S["he_kept"], 1)
                if t.exists():
                    after(dve, S["te_done"], t)
                    v.scalar_tensor_tensor(ge[t.slot][:], te[t.slot][:], 1.0, pe_gu[t.slot][:, 0:I],
                                           ALU.add, ALU.mult).then_inc(S["ge_done"], 1)
                    after(dve, S["ge_done"], t)
                    after(dve, S["he_turned"], t.before(2))
                    v.scalar_tensor_tensor(he[t.slot][:], ge[t.slot][:], 0.5, pe_gu[t.slot][:, I:2 * I],
                                           ALU.mult, ALU.mult).then_inc(S["he_done"], 1)
                if d.exists():
                    after(dve, S["ye_made"], d)
                    landed(dve, ye_out, d.before(2))
                    v.tensor_copy(ye[d.slot][:], pe_y[d.slot]).then_inc(S["ye_done"], 1)

            for_all_steps(dve, TILES, 3, tile_step, 4)

            def last_step(i):
                t, d = i.before(2), i.before(4)
                if d.exists():
                    landed(dve, first_in, d)
                    after(dve, S["both_done"], d)
                    after(dve, S["part2_done"], d.before(2))
                    v.scalar_tensor_tensor(part[d.slot][:], first[d.slot4][:], scal[d.slot4][:, 0:1], both[d.slot4][:],
                                           ALU.mult, ALU.add).then_inc(S["part_done"], 1)
                    landed(dve, second_in, d)
                    after(dve, S["part_done"], d)
                    after(dve, S["total_done"], d.before(2))
                    v.scalar_tensor_tensor(part2[d.slot][:], second[d.slot4][:], scal[d.slot4][:, 1:2], part[d.slot][:],
                                           ALU.mult, ALU.add).then_inc(S["part2_done"], 1)
                    after(dve, S["part2_done"], d)
                    after(dve, S["shared_made"], d)
                    landed(dve, total_out, d.before(2))
                    v.tensor_tensor(total[d.slot][:], pe_y[d.slot], part2[d.slot][:], ALU.add
                                    ).then_inc(S["total_done"], 1)
                if i.exists():
                    after(dve, S["part2_done"], i.before(4))
                    stand(i.slot)
                    v.tensor_copy(scal[i.slot4][:], kept[:, bass.ds(i.number, 1), :].rearrange("p a b -> p (a b)")
                                  ).then_inc(S["scal_done"], 1)
                    after(dve, S["scal_done"], i)
                    landed(dve, x1_in, i)
                    after(dve, S["xn3_turned"], i.before(2))
                    after(dve, S["both_done"], i.before(2))
                    v.tensor_scalar(xn3[i.slot][:], x1_back[i.slot][:], scal[i.slot4][:, 2:3], scal[i.slot4][:, 3:4],
                                    ALU.subtract, ALU.mult).then_inc(S["xn3_done"], 1)
                if t.exists():
                    after(dve, S["tsh_done"], t)
                    v.scalar_tensor_tensor(gsh[t.slot][:], tsh[t.slot][:], 1.0, pe_gu[t.slot][:, 0:I],
                                           ALU.add, ALU.mult).then_inc(S["gsh_done"], 1)
                    after(dve, S["gsh_done"], t)
                    after(dve, S["hsh_turned"], t.before(2))
                    v.scalar_tensor_tensor(hsh[t.slot][:], gsh[t.slot][:], 0.5, pe_gu[t.slot][:, I:2 * I],
                                           ALU.mult, ALU.mult).then_inc(S["hsh_done"], 1)
                if i.exists():
                    after(dve, S["xn3_done"], i)
                    after(dve, S["part_done"], i.before(4))
                    v.tensor_tensor(both[i.slot4][:], x1_back[i.slot][:], xn3[i.slot][:], ALU.add
                                    ).then_inc(S["both_done"], 1)
            for_all_steps(dve, BATCHES, 4, last_step, 4)

        @block.tensor
        def _(pe):
            t = nc.tensor
            t_ = nc.tensor.transpose

            def mm(dst, left, right, first=True, last=True, shared=False):
                return t.matmul(dst, left, right, start=first, stop=last, skip_group_check=shared)

            pe.wait_ge(w_in, 16 * 12)
            pe.wait_ge(setup_p, 1)
            pe.wait_ge(setup_v, 2)
            for c in range(DC):
                mm(b4[:, 0:D], bv_rep[:, c, :], wo_sb[:, c, :], c == 0, False)
            mm(b4[:, 0:D], ones_row[:], wo_b_row[:], False, True)
            mm(b5[:, 0:E], ones_row[:], gate_b_row[:]).then_inc(setup_pe, 1)
            pe.wait_ge(setup_done, 1)
            pe.wait_ge(bias_in, 48)

            def step(i):
                s, o, p = i.before(1), i.before(2), i.before(3)

                def project(dst, w, n, x0, done):
                    for c in range(DC):
                        mm(dst, xc_t[i.slot][:, x0 + c, :], w[:, c, :], c == 0, False)
                    mm(dst, ones3[:], bias3[:, n, :], False, True).then_inc(done, 1)

                def halves(b, r, c):
                    g = slice(64 * (r % 2), 64 * (r % 2) + 64)
                    return q_t[b.slot][g, 2 * c + r // 2, :], k_t[b.slot][g, 2 * c + r // 2, :]

                def scores(b, pair):
                    for c in range(HC):
                        for r in (pair, pair + 1):
                            q, k = halves(b, r, c)
                            m = mm(ps_s[:, r, c * P:(c + 1) * P], q, k)
                            if c == HC - 1:
                                m.then_inc(S["scores_made"], 1)

                if s.exists():
                    after(pe, S["q_kept"], s)
                    after(pe, S["k_kept"], s)
                    after(pe, S["probs_done"], s.before(1), 4)
                    scores(s, 0)
                if p.exists():
                    after(pe, S["chosen_bf_done"], p)
                    after(pe, S["seen_done"], p.before(1))
                    mm(ps_rank, earlier[:], chosen_bf[p.slot][:], True, False)
                    mm(ps_rank, ones_bf[:], seen[:], False, True).then_inc(S["rank_made"], 1)
                if s.exists():
                    scores(s, 2)
                if i.exists():
                    after(pe, S["xn_done"], i)
                    landed(pe, c_in, i)
                    after(pe, S["k_kept"], s)
                    for c in range(DC):
                        t.transpose(ps_xc[:, c, :], xn[i.slot][:, c * P:(c + 1) * P], ident[:])
                    for c in range(DC):
                        m = t.transpose(ps_xc[:, DC + c, :], c_sb[i.slot][:, c * P:(c + 1) * P], ident[:])
                    m.then_inc(S["xc_turned"], 1)
                if o.exists():
                    after(pe, S["pv_kept"], o)
                    after_first(pe, (S["rank_done"], p), (S["q_lo_done"], s))
                    for c in range(HC):
                        m = t.transpose(b7[:, c * P:(c + 1) * P], o_un[o.slot][:, c, :], ident[:])
                    m.then_inc(S["o_turned"], 1)
                if s.exists():
                    for c in range(DC):
                        m = mm(ps_v, xc_t[s.slot][:, DC + c, :], wv_sb[:, c, :], c == 0, c == DC - 1)
                    m.then_inc(S["v_made"], 1)
                if i.exists():
                    after(pe, S["xc_kept"], i)
                    after_first(pe, (S["o_done"], o), (S["q_lo_done"], s))
                    project(ps_q, wq_sb, 0, 0, S["q_made"])
                if o.exists():
                    after(pe, S["o_done"], o)
                    after_first(pe, (S["v_done"], s), (S["max_kept"], o))
                    for c in range(DC):
                        m = t.transpose(ps_ot[:, c, :], o_sb[o.slot][:, c * P:(c + 1) * P], ident[:])
                    m.then_inc(S["ot_made"], 1)
                if i.exists():
                    project(ps_k, wk_sb, 1, DC, S["k_made"])
                if s.exists():
                    after(pe, S["max_lo_done"], s)
                    after_first(pe, (S["ot_kept"], o), (S["v_done"], s))
                    t.transpose(ps_mt, max_parts[s.slot][:].rearrange("p r j -> p (r j)"), ident_bf[:]
                                ).then_inc(S["max_turned"], 1)
                if o.exists():
                    after(pe, S["ot_kept"], o)
                    after(pe, S["pv_kept"], o)
                    for c in range(DC):
                        m = mm(ps_wo, o_t[o.slot][:, c, :], wo_sb[:, c, :], c == 0, c == DC - 1)
                    m.then_inc(S["wo_made"], 1)
                if s.exists():
                    after(pe, S["max_kept"], s)
                    for pair in (0, 2):
                        for c in range(HC):
                            for r in (pair, pair + 1):
                                q, k = halves(s, r, c)
                                mm(ps_s[:, r, c * P:(c + 1) * P], k, q, c == 0, False, True)
                            for r in (pair, pair + 1):
                                g = slice(32 * r, 32 * r + 32)
                                m = mm(ps_s[:, r, c * P:(c + 1) * P], pick[g, c, :], max_t[s.slot][g, :],
                                       False, True, True)
                                if c == HC - 1:
                                    m.then_inc(S["shifted_made"], 1)
                if i.exists():
                    after(pe, S["q_lo_done"], i)
                    after(pe, S["max_kept"], s)
                    for c in range(H // 2):
                        m = t.transpose(ps_qt[:, c, :], q_parts[i.slot][:, 2 * c:2 * c + 2].rearrange(
                            "p h a b w -> p (h a b w)"), ident_half[:])
                    m.then_inc(S["q_turned"], 1)
                if o.exists():
                    after(pe, S["xn2_done"], o)
                    for c in range(DC):
                        m = t.transpose(ps_x2[:, c, :], xn2[o.slot4][:, c * P:(c + 1) * P], ident[:])
                    m.then_inc(S["x2_turned"], 1)
                if i.exists():
                    after(pe, S["k_lo_done"], i)
                    for c in range(H // 2):
                        m = t.transpose(ps_kt[:, c, :], k_parts[i.slot][:, 2 * c:2 * c + 2].rearrange(
                            "p h a b w -> p (h a b w)"), ident_half[:])
                    m.then_inc(S["k_turned"], 1)
                if o.exists():
                    after(pe, S["x2_kept"], o)
                    after_first(pe, (S["q_lo_done"], i), (S["o_done"], o))
                    for c in range(DC):
                        m = mm(ps_router, xn2_t[o.slot][:, c, :], router_sb[:, c, :], c == 0, c == DC - 1)
                    m.then_inc(S["logits_made"], 1)
                if s.exists():
                    after(pe, S["probs_done"], s, 4)
                    after(pe, S["v_done"], s)
                    after_first(pe, (S["x2_kept"], o))
                    for c in range(HC):
                        for r in range(4):
                            g = slice(32 * r, 32 * r + 32)
                            m = mm(ps_pv[g, c, :], v_sb[s.slot][:, 4 * c + r, :], probs[s.slot][:, r, c, :])
                    m.then_inc(S["pv_made"], 1)

            for_all_steps(pe, BATCHES, 3, step, 4)

            pe.wait_ge(S["seen_done"], BATCHES)
            pe.wait_ge(S["o_done"], BATCHES)
            pe.wait_ge(S["k_kept"], BATCHES)
            mm(b5[:, 0:E], ones_bf[:], seen[:]).then_inc(S["counted"], 1)
            pe.wait_ge(S["table"], TABLE_STEPS)
            pe.wait_ge(S["pv_kept"], BATCHES)
            pe.wait_ge(S["rank_done"], BATCHES)
            for n, table in enumerate((b6, b7)):
                for c in range(TC):
                    m = mm(table[0:1, c * P:(c + 1) * P], table_col[:, n, c:c + 1], ident[:])
            m.then_inc(S["tables_turned"], 1)
            pe.wait_ge(w_in2, 32)
            pe.wait_ge(S["tables_kept"], 2)
            pe.wait_ge(S["max_kept"], BATCHES)

            experts_read = []

            def tile_step(i):
                t, h, d = i.before(1), i.before(2), i.before(3)
                if i.slot4 == 0:
                    turn = i.turn if i.offset == 0 else i.turn + i.offset // 4
                    word = read_registers(mybir.EngineType.PE, turn_tab[0:1, bass.ds(turn, 1)], 16 ** 6 - 1)[0]
                    experts_read[:] = [(word >> 4 * n) & (E - 1) for n in range(6)]
                e_t, e_d = experts_read[i.slot4 + 2], experts_read[i.slot4]
                if i.exists():
                    landed(pe, xe_in, i)
                    after(pe, S["xe_kept"], i.before(2))
                    for c in range(DC):
                        m = t_(pe_xe[i.slot][:, c, :], xe[i.slot4][:, c * P:(c + 1) * P], ident[:])
                    m.then_inc(S["xe_turned"], 1)
                if t.exists():
                    after(pe, S["xe_kept"], t)
                    after(pe, S["he_done"], t.before(2))
                    for c in range(DC):
                        m = mm(pe_gu[t.slot], xe_t[t.slot][:, c, :],
                               eg_sb[:, bass.ds(e_t, 1), c, :].rearrange("p a n -> p (a n)"), c == 0, c == DC - 1)
                    m.then_inc(S["ge_made"], 1)
                if h.exists():
                    after(pe, S["he_done"], h)
                    after(pe, S["he_kept"], h.before(2))
                    t_(pe_h[h.slot], he[h.slot][:], ident[:]).then_inc(S["he_turned"], 1)
                if d.exists():
                    after(pe, S["he_kept"], d)
                    after(pe, S["ye_done"], d.before(2))
                    mm(pe_y[d.slot], he_t[d.slot][:], ed_sb[:, bass.ds(e_d, 1), :].rearrange("p a n -> p (a n)")
                       ).then_inc(S["ye_made"], 1)

            for_all_steps(pe, TILES, 3, tile_step, 4)

            pe.wait_ge(S["he_done"], TILES)
            pe.wait_ge(S["he_kept"], TILES)
            pe.wait_ge(S["ye_done"], TILES)

            def last_step(i):
                t, h, d = i.before(1), i.before(3), i.before(4)
                if d.exists():
                    after(pe, S["hsh_kept"], d)
                    after(pe, S["total_done"], d.before(2))
                    mm(pe_y[d.slot], hsh_t[d.slot][:], sd_sb[:]).then_inc(S["shared_made"], 1)
                if h.exists():
                    after(pe, S["hsh_done"], h)
                    after(pe, S["hsh_kept"], h.before(2))
                    t_(pe_h[h.slot], hsh[h.slot][:], ident[:]).then_inc(S["hsh_turned"], 1)
                if t.exists():
                    after(pe, S["xn3_kept"], t)
                    after(pe, S["hsh_done"], t.before(2))
                    for c in range(DC):
                        m = mm(pe_gu[t.slot], xn3_t[t.slot][:, c, :], gu_sb[:, c, :], c == 0, c == DC - 1)
                    m.then_inc(S["gsh_made"], 1)
                if i.exists():
                    after(pe, S["xn3_done"], i)
                    after(pe, S["xn3_kept"], i.before(2))
                    for c in range(DC):
                        m = t_(pe_xe[i.slot][:, c, :], xn3[i.slot][:, c * P:(c + 1) * P], ident[:])
                    m.then_inc(S["xn3_turned"], 1)

            for_all_steps(pe, BATCHES, 4, last_step, 4)


def kernel(**inputs):
    import numpy as np
    import concourse.bacc as bacc
    from concourse.bass_utils import run_bass_kernel_spmd

    a = {name: np.asarray(value) for name, value in inputs.items()}
    x = a["x"]
    rows = lambda n: a[n].reshape(1, -1)
    turned = lambda n: np.ascontiguousarray(a[n].T)
    D = x.shape[-1]
    arrays = {
        "x": x.reshape(-1, D), "ctx": a["ctx_1024"].reshape(-1, D),
        "wq_t": turned("L0_xattn_wq_w"), "wq_b": rows("L0_xattn_wq_b"),
        "wk_t": turned("L0_xattn_wk_w"), "wk_b": rows("L0_xattn_wk_b"),
        "wv_t": turned("L0_xattn_wv_w"), "wv_b": np.ascontiguousarray(a["L0_xattn_wv_b"].reshape(-1, P).T),
        "wo_t": turned("L0_xattn_wo_w"), "wo_b": rows("L0_xattn_wo_b"),
        "gate_w": a["L0_ffn_gate_w"], "gate_b": rows("L0_ffn_gate_b"),
        "shared_gu": np.concatenate([a["L0_ffn_shared_wg"], a["L0_ffn_shared_wu"]], axis=1),
        "shared_d": a["L0_ffn_shared_wd"],
        "experts_gu": np.concatenate([a["L0_ffn_experts_wg"], a["L0_ffn_experts_wu"]], axis=2),
        "experts_d": a["L0_ffn_experts_wd"],
    }
    nc = bacc.Bacc("TRN2", target_bir_lowering=False, num_devices=1)
    arrays = {f"in_{name}": np.ascontiguousarray(value) for name, value in arrays.items()}
    operands = [nc.dram_tensor(name, value.shape, fp32, kind="ExternalInput").ap() for name, value in arrays.items()]
    out = nc.dram_tensor("out", (x.shape[0] * x.shape[1], D), fp32, kind="ExternalOutput").ap()
    xattn_moe_kernel(nc, *operands, out)
    result = run_bass_kernel_spmd(nc, [arrays], core_ids=[0])
    return result.results[0]["out"].reshape(x.shape)
```

```python
import concourse.bass as bass
from concourse import mybir
from contextlib import ExitStack

fp32 = mybir.dt.float32
fp16 = mybir.dt.float16
bf16 = mybir.dt.bfloat16
u32 = mybir.dt.uint32
i32 = mybir.dt.int32
ALU = mybir.AluOpType
ACT = mybir.ActivationFunctionType
AX = mybir.AxisListType

P = 128
H, DH = 16, 16
TOP_K = 2
LN_EPS = 1e-5
SIGMOID_ONE = 17.5


class Batch:

    def __init__(self, turn, offset, batches, unroll=2):
        self.turn, self.offset, self.batches, self.unroll = turn, offset, batches, unroll
        self.number = turn * unroll + offset
        self.slot = offset % 2
        self.slot4 = offset % 4

    def before(self, n):
        return Batch(self.turn, self.offset - n, self.batches, self.unroll)

    def exists(self):
        return not isinstance(self.number, int) or 0 <= self.number < self.batches


def after(engine, signal, batch, each=1, nth=None):
    if batch.exists():
        nth = each if nth is None else nth
        engine.wait_ge(signal, batch.turn * (batch.unroll * each) + batch.offset * each + nth)


def landed(engine, signals, batch):
    if batch.exists():
        n = len(signals)
        engine.wait_ge(signals[batch.offset % n],
                       batch.turn * (batch.unroll // n * 16) + (batch.offset // n + 1) * 16)


def after_first(engine, *events):
    for signal, batch in events:
        if batch.exists():
            after(engine, signal, batch)
            return


def for_all_steps(engine, batches, depth, step, unroll=2):
    peeled = 2 * unroll
    for i in range(peeled):
        step(Batch(0, i, batches, unroll))
    with engine.Fori(peeled // unroll, batches // unroll - 1) as turn:
        for u in range(unroll):
            step(Batch(turn, u, batches, unroll))
    for i in range(batches - unroll, batches + depth):
        step(Batch(0, i, batches, unroll))


def xattn_moe_kernel(nc, x, ctx_in, wq_t, wq_b, wk_t, wk_b, wv_t, wv_b, wo_t, wo_b,
                     gate_w, gate_b, shared_gu, shared_d, experts_gu, experts_d, out):
    TOKENS, D = x.shape
    BATCHES = TOKENS // P
    E = gate_w.shape[1]
    I = shared_d.shape[0]
    DC = D // P
    HC = 4
    REGION = TOKENS
    TILES = TOP_K * TOKENS // P + E
    TC = -(-TILES // P)
    TURN = 8
    TURNS = TILES // TURN + 1
    assert E & (E - 1) == 0, "an expert's digit has whole bits"
    DIGITS = (TURN + 2) // 2
    DIGIT_BITS = (E - 1).bit_length()
    FILLS = 8
    TABLE_STEPS = 16
    STAIR_STEPS = 4

    xs_dram = nc.dram_tensor("expert_in", [E * REGION, D], fp32).ap()
    ys_dram = nc.dram_tensor("expert_out", [TILES * P, D], fp32).ap()
    x1_dram = nc.dram_tensor("after_attention", [TOKENS, D], fp32).ap()

    with ExitStack() as stack:
        def sb(name, shape, dt=fp32):
            return stack.enter_context(nc.sbuf_tensor(name, shape, dt))

        def pb(name, shape, dt=fp32):
            return stack.enter_context(nc.psum_tensor(name, shape, dt))

        def sem(name):
            return stack.enter_context(nc.semaphore(name))

        wq_sb = sb("wq_sb", [P, DC, D])
        wk_sb = sb("wk_sb", [P, DC, D])
        wv_sb = sb("wv_sb", [P, DC, D])
        wo_sb = sb("wo_sb", [P, DC, D])
        router_sb = sb("router_sb", [P, DC, E])
        gu_sb = sb("gu_sb", [P, DC, 2 * I])
        sd_sb = sb("sd_sb", [P, D])
        eg_sb = sb("eg_sb", [P, E, DC, 2 * I])
        ed_sb = sb("ed_sb", [P, E, D])
        bias_row = sb("bias_row", [1, 2, D])
        bias_left = sb("bias_left", [1, 2, D])
        bias_parts = sb("bias_parts", [1, 3, 2, D], bf16)
        bias3 = sb("bias3", [3, 2, D], bf16)
        wo_b_row = sb("wo_b_row", [1, D])
        gate_b_row = sb("gate_b_row", [1, E])
        bv_col = sb("bv_col", [P, DC])
        bv_rep = sb("bv_rep", [P, DC, P])
        attn_bias = sb("attn_bias", [P, D])
        gate_bias = sb("gate_bias", [P, E])
        ones_row = sb("ones_row", [1, P])
        ones3 = sb("ones3", [3, P], bf16)
        ones_bf = sb("ones_bf", [P, P], bf16)
        col_iota = sb("col_iota", [P, P])
        row_int = sb("row_int", [P, 1], i32)
        row_int4 = sb("row_int4", [P, 1], i32)
        row_iota = sb("row_iota", [P, 1])
        row_mod4 = sb("row_mod4", [P, 1])
        ident = sb("ident", [P, P])
        ident_bf = sb("ident_bf", [P, P], bf16)
        ident_half = sb("ident_half", [P, P], fp16)
        earlier = sb("earlier", [P, P], bf16)
        pick = sb("pick", [P, HC, P], bf16)
        minus_half = sb("minus_half", [P, 1])
        region_start = sb("region_start", [P, E])
        slot_all = sb("slot_all", [P, BATCHES, TOP_K])
        expert_all = sb("expert_all", [P, BATCHES, TOP_K])
        kept = sb("kept", [P, BATCHES, 4])
        gate_all = kept[:, :, 0:TOP_K]
        seen = sb("seen", [P, E], bf16)
        def two(name, shape, dt=fp32):
            return [sb(f"{name}{n}", shape, dt) for n in range(2)]

        spare_pool, spare_dve = two("spare_pool", [P, 1]), two("spare_dve", [P, 1])
        x_sb = two("x_sb", [P, D])
        c_sb = two("c_sb", [P, D])
        xn = two("xn", [P, D])
        x_res = two("x_res", [P, D])
        stats1, stats2 = two("stats1", [P, 6]), two("stats2", [P, 6])
        mv1, mv2 = two("mv1", [P, 3]), two("mv2", [P, 3])
        ve1, ve2 = two("ve1", [P, 1]), two("ve2", [P, 1])
        xc_t = two("xc_t", [P, 2 * DC, P])
        q_parts = two("q_parts", [P, H, 2, 2, DH], fp16)
        k_parts = two("k_parts", [P, H, 2, 2, DH], fp16)
        q_t = two("q_t", [P, H // 2, P], fp16)
        k_t = two("k_t", [P, H // 2, P], fp16)
        v_sb = two("v_sb", [P, H, 2 * DH])
        neg_max = two("neg_max", [P, 4, HC])
        max_parts = two("max_parts", [P, 4, 32], bf16)
        max_t = two("max_t", [P, P], bf16)
        probs = two("probs", [P, 4, HC, P])
        o_un = two("o_un", [P, HC, P])
        o_rec = two("o_rec", [P, HC, 4])
        o_sb = two("o_sb", [P, D])
        o_t = two("o_t", [P, DC, P])
        x1 = two("x1", [P, D])
        xn2 = [sb(f"xn2_{n}", [P, D]) for n in range(4)]
        xn2_t = two("xn2_t", [P, DC, P])
        key = two("key", [P, E])
        top_v = two("top_v", [P, 8])
        top_i = two("top_i", [P, 8], u32)
        chosen = two("chosen", [P, TOP_K, E])
        chosen_bf = two("chosen_bf", [P, E], bf16)
        rank = two("rank", [P, E])
        rank2 = two("rank2", [P, TOP_K, E])
        slot_int = [sb(f"slot_int{n}", [P, TOP_K], u32) for n in range(4)]

        rows_of = sb("rows_of", [P, E])
        count_int = sb("count_int", [P, E], i32)
        tiles_int = sb("tiles_int", [P, E], i32)
        tiles = sb("tiles", [P, E])
        tiles_end = sb("tiles_end", [P, E])
        final = sb("final", [P, E])
        full = sb("full", [P, E])
        back = sb("back", [P, E])
        edge = sb("edge", [P, 2, E + 1])
        jump = sb("jump", [P, 2, E + 1])
        out_shift = sb("out_shift", [P, E + 1])
        shift_part = sb("shift_part", [P, BATCHES * TOP_K])
        shifted = sb("shifted", [P, BATCHES * TOP_K])
        ones_e = sb("ones_e", [P, E])
        tile_iota = sb("tile_iota", [P, TC])
        last_tile = sb("last_tile", [P, 1])
        per_tile = sb("per_tile", [P, 3, TC, E])
        sums = sb("sums", [P, 3, TC])
        table_col = sb("table_col", [P, 2, TC])
        turn_tab = sb("turn_tab", [1, 2 * TURNS], i32)
        packed = [sb(f"packed{n}", [1, TURNS, 2]) for n in range(2)]
        expert_row = sb("expert_row", [1, TURN * (TURNS + 2)])
        row_tab = sb("row_tab", [1, TC * P], i32)
        zeros = sb("zeros", [P, D])
        gate_sum = sb("gate_sum", [P, BATCHES])
        xe = [sb(f"xe{n}", [P, D]) for n in range(4)]
        xe_t = two("xe_t", [P, DC, P])
        te = two("te", [P, I])
        ge = two("ge", [P, I])
        he = two("he", [P, I])
        he_t = two("he_t", [P, P])
        ye = two("ye", [P, D])
        out_row = sb("out_row", [P, BATCHES * TOP_K], u32)
        gather_row = [sb(f"gather_row{n}", [P, TOP_K], u32) for n in range(4)]

        def four(name, shape):
            return [sb(f"{name}{n}", shape) for n in range(4)]

        first, second = four("first", [P, D]), four("second", [P, D])
        x1_back = four("x1_back", [P, D])
        centred = two("centred", [P, D])
        xn3, xn3_t = two("xn3", [P, D]), two("xn3_t", [P, DC, P])
        both = four("both", [P, D])
        tsh, gsh, hsh, hsh_t = (two(name, [P, I]) for name in ("tsh", "gsh", "hsh", "hsh_t"))
        part, part2 = two("part", [P, D]), two("part2", [P, D])
        total = two("total", [P, D])

        ps_s = pb("ps_s", [P, 4, 512])
        b4, b5, b6, b7 = (pb(f"b{n}", [P, 512]) for n in (4, 5, 6, 7))
        ps_ot = b4[:, 0:D].rearrange("p (c t) -> p c t", c=DC)
        ps_mt = b4[:, :].bitcast(bf16)[:, 0:P]
        ps_v = b4[:, 0:D]
        ps_qt = b4[:, :].bitcast(fp16).rearrange("p (c t) -> p c t", c=H // 2)
        ps_xc = b5[:, :].rearrange("p (c t) -> p c t", c=2 * DC)
        ps_kt = b5[:, :].bitcast(fp16).rearrange("p (c t) -> p c t", c=H // 2)
        ps_wo = b6[:, 0:D]
        ps_x2 = b7[:, 0:D].rearrange("p (c t) -> p c t", c=DC)
        ps_pv = b6[:, :].rearrange("p (c t) -> p c t", c=HC)
        ps_o = b7[:, :].rearrange("p (c r w) -> p c r w", c=HC, r=4)
        ps_q, ps_k = b7[:, 0:D], b5[:, 0:D]
        ps_router = b6[:, 0:E]
        ps_rank = b7[:, E:2 * E]

        pe_xe = [ps_s[:, n, 0:D].rearrange("p (c t) -> p c t", c=DC) for n in range(2)]
        pe_gu = [ps_s[:, 2 + n, 0:2 * I] for n in range(2)]
        pe_h = [b4[:, 0:P], b5[:, 0:P]]
        pe_y = [b6[:, 0:D], b7[:, 0:D]]

        w_in, w_in2 = sem("w_in"), sem("w_in2")
        consts, bias_split, bias_in, setup_v, setup_p, setup_pe, setup_done = (
            sem(n) for n in ("consts", "bias_split", "bias_in", "setup_v", "setup_p", "setup_pe", "setup_done"))
        zeroed = sem("zeroed")
        stood = [sem(f"stood{n}") for n in range(2)]
        x_in = [sem(f"x_in{n}") for n in range(2)]
        x1_out = [sem(f"x1_out{n}") for n in range(2)]
        c_in = [sem(f"c_in{n}") for n in range(2)]
        names = """stats1_done mv1_done ve1_done rstd1_done xn_done x_res_done
            xc_turned xc_kept q_made q_hi_done q_lo_done k_made k_hi_done k_lo_done
            q_turned q_kept k_turned k_kept v_made v_done
            scores_made max_taken max_hi_done max_lo_done max_turned max_kept shifted_made
            probs_done pv_made pv_kept o_turned rec_done o_done
            ot_made ot_kept wo_made x1_done stats2_done mv2_done ve2_done rstd2_done xn2_done
            x2_turned x2_kept logits_made biased_done key_done topv_done topi_done expert_done
            chosen_done chosen_bf_done gate_exp norm_kept rank_made seen_done
            rank_done rank2_done slotf_done slot_done
            sent negated counted packed_done table tables_turned tables_kept shift_done gate_done
            xe_turned xe_kept ge_made te_done ge_done he_done he_turned he_kept ye_made ye_done
            centred_done xn3_done both_done xn3_turned xn3_kept gsh_made tsh_done gsh_done hsh_done
            hsh_turned hsh_kept shared_made gather_row_done part_done part2_done
            total_done""".split()
        S = {n: sem(n) for n in names}
        xe_in = [sem(f"xe_in{n}") for n in range(4)]
        ye_out, total_out = ([sem(f"{name}{n}") for n in range(2)] for name in ("ye_out", "total_out"))
        x1_in, first_in, second_in = (
            [sem(f"{name}{n}") for n in range(4)] for name in ("x1_in", "first_in", "second_in"))

        block = stack.enter_context(nc.Block())

        def rows(dram, batch):
            return dram[bass.ds(batch.number * P, P), :]

        def of_batch(batch, n):
            return kept[:, bass.ds(batch.number, 1), n:n + 1].rearrange("p a b -> p (a b)")

        def read_registers(engine, numbers, largest):
            _, values = nc.values_load_multi_w_load_instructions(
                numbers, engines=[engine], min_val=0, max_val=largest)
            return list(values)

        @block.sync
        def _(sp):
            chunked = lambda w: w.rearrange("(c p) n -> p c n", p=P)
            for dst, src in ((wq_sb[:], chunked(wq_t)), (wk_sb[:], chunked(wk_t)),
                             (bias_row[:, 0, :], wq_b), (bias_row[:, 1, :], wk_b),
                             (wv_sb[:], chunked(wv_t)), (wo_sb[:], chunked(wo_t)),
                             (bv_col[:], wv_b), (wo_b_row[:], wo_b), (gate_b_row[:], gate_b),
                             (router_sb[:], chunked(gate_w)),
                             (gu_sb[:], chunked(shared_gu)), (sd_sb[:], shared_d)):
                sp.dma_start(dst, src).then_inc(w_in, 16)
            for b in range(2):
                sp.dma_start(x_sb[b][:], x[b * P:(b + 1) * P, :]).then_inc(x_in[b], 16)
            sp.dma_start(c_sb[0][:], ctx_in[0:P, :]).then_inc(c_in[0], 16)
            sp.wait_ge(bias_split, 5)
            for n in range(3):
                sp.dma_start(bias3[n:n + 1, :, :], bias_parts[:, n, :, :]).then_inc(bias_in, 16)

            def fill(n):
                sp.wait_ge(consts, 2)
                for e in range(2 * E * n // FILLS, 2 * E * (n + 1) // FILLS):
                    if e < E:
                        sp.dma_start(xs_dram[e * REGION:e * REGION + P, :], zeros[:]).then_inc(zeroed, 16)
                    else:
                        sp.dma_start(eg_sb[:, e - E], experts_gu[e - E].rearrange("(c p) n -> p c n", p=P)
                                     ).then_inc(w_in2, 16)
                        sp.dma_start(ed_sb[:, e - E], experts_d[e - E]).then_inc(w_in2, 16)

            def step(i):
                b = i.before(-1)
                if b.exists():
                    after(sp, S["xc_turned"], b.before(2))
                    sp.dma_start(c_sb[b.slot][:], rows(ctx_in, b)).then_inc(c_in[b.slot], 16)
                if isinstance(i.number, int) and i.number < FILLS:
                    fill(i.number)
                b = i.before(2)
                if b.exists():
                    after(sp, S["x1_done"], b)
                    sp.dma_start(rows(x1_dram, b), x1[b.slot][:]).then_inc(x1_out[b.slot], 16)
                b = i.before(-2)
                if b.exists():
                    after(sp, S["x_res_done"], i)
                    after(sp, S["xn_done"], i)
                    sp.dma_start(x_sb[b.slot][:], rows(x, b)).then_inc(x_in[b.slot], 16)

            for_all_steps(sp, BATCHES, 2, step, 4)

            for n in range(2):
                sp.wait_ge(x1_out[n], BATCHES // 2 * 16)
            sp.wait_ge(S["sent"], 32 * BATCHES)
            sp.wait_ge(S["tables_kept"], 2)

            first_rows = []

            def tile_step(i):
                if i.slot4 == 0:
                    first_rows[:] = read_registers(mybir.EngineType.SP, row_tab[0:1, bass.ds(i.number, 4)],
                                                   E * REGION - P)
                after(sp, S["xe_turned"], i.before(4))
                sp.dma_start(xe[i.slot4][:], xs_dram[bass.ds(first_rows[i.slot4], P), :]
                             ).then_inc(xe_in[i.slot4], 16)

            for_all_steps(sp, TILES, 0, tile_step, 4)

            def last_step(i):
                if i.exists():
                    after(sp, S["both_done"], i.before(4))
                    sp.dma_start(x1_back[i.slot4][:], rows(x1_dram, i)).then_inc(x1_in[i.slot4], 16)
                o = i.before(5)
                if o.exists():
                    after(sp, S["total_done"], o)
                    sp.dma_start(rows(out, o), total[o.slot][:]).then_inc(total_out[o.slot], 16)

            for_all_steps(sp, BATCHES, 5, last_step, 4)
            for n in range(2):
                sp.wait_ge(total_out[n], BATCHES // 2 * 16)

        @block.gpsimd
        def _(pool):
            g = nc.gpsimd

            g.iota(col_iota[:], pattern=[[1, P]], base=0, channel_multiplier=0,
                   allow_small_or_imprecise_dtypes=True)
            g.iota(row_int[:], pattern=[[0, 1]], base=0, channel_multiplier=1)
            g.iota(region_start[:], pattern=[[REGION, E]], base=0, channel_multiplier=0,
                   allow_small_or_imprecise_dtypes=True)
            g.memset(minus_half[:], -0.5)
            g.memset(ones_row[:], 1.0)
            g.memset(ones3[:], 1.0)
            g.memset(ones_bf[:], 1.0)
            g.memset(seen[:], 0.0)
            for n in range(2):
                g.memset(v_sb[n][:, :, DH:DH + 1], 1.0)
                g.memset(v_sb[n][:, :, DH + 1:], 0.0)
                m = g.memset(max_parts[n][:], 0.0)
            m.then_inc(consts, 1)
            g.iota(tile_iota[:], pattern=[[P, TC]], base=0, channel_multiplier=1,
                   allow_small_or_imprecise_dtypes=True)
            g.memset(zeros[:], 0.0)
            g.memset(expert_row[:], 0.0)
            g.memset(ones_e[:], 1.0).then_inc(consts, 1)
            pool.wait_ge(consts, 2)

            def stand(b, k):
                after(pool, stood[k], b.before(1))
                g.tensor_tensor(spare_pool[k][:], minus_half[:], minus_half[:], ALU.add).then_inc(stood[k], 1)

            def norm_pow(b, source, target, ready, free, done):
                after(pool, ready, b)
                after(pool, free, b.before(2))
                g.tensor_tensor(target[b.slot][:, 2:3], source[b.slot][:], minus_half[:],
                                ALU.pow).then_inc(done, 1)

            def scatter_free(b, k):
                if k == 0 and isinstance(b.number, int) and b.number == 0:
                    pool.wait_ge(zeroed, 16 * E)
                after(pool, S["slot_done"], b)
                if k:
                    after(pool, S["sent"], b, 32, 16)
                else:
                    after(pool, S["sent"], b.before(1), 32)

            def scatter(b, k):
                g.indirect_dma_start(
                    xs_dram[:, :], bass.IndirectOffsetOnAxis(ap=slot_int[b.slot4][:, k:k + 1], axis=0),
                    xn2[b.slot4][:], None).then_inc(S["sent"], 16)

            norm_pow(Batch(0, 0, BATCHES), ve1, mv1, S["ve1_done"], S["xn_done"], S["rstd1_done"])

            def step(i):
                o, p, q, n = i.before(2), i.before(3), i.before(4), i.before(-1)
                if q.exists():
                    scatter_free(q, 0)
                    stand(q, 0)
                    scatter(q, 0)
                if n.exists():
                    norm_pow(n, ve1, mv1, S["ve1_done"], S["xn_done"], S["rstd1_done"])
                if q.exists():
                    scatter_free(q, 1)
                    stand(q, 1)
                    scatter(q, 1)
                if o.exists():
                    norm_pow(o, ve2, mv2, S["ve2_done"], S["norm_kept"], S["rstd2_done"])
                if i.exists():
                    if isinstance(i.number, int) and i.number == 0:
                        pool.wait_ge(setup_done, 1)
                    landed(pool, x_in, i)
                    after(pool, S["x1_done"], i.before(2))
                    g.tensor_tensor(x_res[i.slot][:], x_sb[i.slot][:], attn_bias[:],
                                    ALU.add).then_inc(S["x_res_done"], 1)
                if p.exists():
                    after(pool, S["rank_made"], p)
                    after(pool, S["seen_done"], p.before(1))
                    g.tensor_tensor(seen[:], seen[:], chosen_bf[p.slot][:],
                                    ALU.add).then_inc(S["seen_done"], 1)

            for_all_steps(pool, BATCHES, 4, step, 4)

            pool.wait_ge(S["table"], TABLE_STEPS + STAIR_STEPS)
            pool.wait_ge(S["slot_done"], BATCHES)
            slots = slot_all[:].rearrange("p b k -> p (b k)")
            g.tensor_copy(shifted[:], slots).then_inc(S["shift_done"], 1)
            for n in range(2 * E):
                at = (slice(None), n % 2, slice(n // 2, n // 2 + 1))
                pool.wait_ge(S["shift_done"], 2 * n + 1)
                g.tensor_scalar(shift_part[:], slots, edge[at], jump[at], ALU.is_ge, ALU.mult).then_inc(S["shift_done"], 1)
                pool.wait_ge(S["shift_done"], 2 * n + 2)
                g.tensor_tensor(shifted[:], shifted[:], shift_part[:], ALU.add).then_inc(S["shift_done"], 1)
            pool.wait_ge(S["shift_done"], 4 * E + 1)
            g.tensor_copy(out_row[:], shifted[:]).then_inc(S["shift_done"], 1)

            pool.wait_ge(S["shift_done"], 4 * E + 2)
            for n in range(2):
                pool.wait_ge(ye_out[n], TILES // 2 * 16)

            def rows_for_gather(b):
                landed(pool, first_in, b.before(4))
                landed(pool, second_in, b.before(4))
                g.tensor_copy(gather_row[b.slot4][:], out_row[:, bass.ds(b.number * TOP_K, TOP_K)]
                              ).then_inc(S["gather_row_done"], 1)

            rows_for_gather(Batch(0, 0, BATCHES, 4))

            def last_step(i):
                n = i.before(-1)
                after(pool, S["gather_row_done"], i)
                after(pool, S["part2_done"], i.before(4))
                if n.exists():
                    rows_for_gather(n)
                for k, (dst, signal) in enumerate(((first, first_in), (second, second_in))):
                    g.indirect_dma_start(dst[i.slot4][:], None, ys_dram[:, :], bass.IndirectOffsetOnAxis(
                        ap=gather_row[i.slot4][:, k:k + 1], axis=0)).then_inc(signal[i.slot4], 16)

            for_all_steps(pool, BATCHES, 0, last_step, 4)

        @block.scalar
        def _(act):
            a = nc.scalar
            def copy(dst, src):
                return a.activation(dst, src, ACT.Copy)

            act.wait_ge(setup_v, 1)

            def step(i):
                s, o, p = i.before(1), i.before(2), i.before(3)

                def exps(pair):
                    after(act, S["shifted_made"], s, 4, pair + 2)
                    after(act, S["pv_made"], s.before(2))
                    a.activation(probs[s.slot][:, pair:pair + 2, :, :],
                                 ps_s[:, pair:pair + 2, :].rearrange("p r (c t) -> p r c t", c=HC),
                                 ACT.Exp, scale=DH ** -0.5).then_inc(S["probs_done"], 1)

                def twice(ps):
                    return ps.rearrange("p (h w) -> p h w", h=H).unsqueeze(2).to_broadcast([P, H, 2, DH])

                if o.exists():
                    after(act, S["pv_made"], o)
                    after(act, S["o_turned"], o.before(2))
                    copy(o_un[o.slot][:], ps_pv).then_inc(S["pv_kept"], 1)
                if p.exists():
                    after(act, S["x2_turned"], p)
                    after(act, S["logits_made"], p.before(2))
                    copy(xn2_t[p.slot][:], ps_x2).then_inc(S["x2_kept"], 1)
                if i.exists():
                    after(act, S["xc_turned"], i)
                    after(act, S["v_made"], i.before(2))
                    copy(xc_t[i.slot][:], ps_xc).then_inc(S["xc_kept"], 1)
                if s.exists():
                    after(act, S["v_made"], s)
                    after(act, S["pv_made"], s.before(2))
                    copy(v_sb[s.slot][:, :, 0:DH], ps_v.rearrange("p (h w) -> p h w", h=H)
                         ).then_inc(S["v_done"], 1)
                if i.exists():
                    after(act, S["q_made"], i)
                    after(act, S["q_turned"], i.before(2))
                    copy(q_parts[i.slot][:, :, :, 0, :], twice(ps_q)).then_inc(S["q_hi_done"], 1)
                if o.exists():
                    after(act, S["ot_made"], o)
                    after(act, S["wo_made"], o.before(2))
                    copy(o_t[o.slot][:], ps_ot).then_inc(S["ot_kept"], 1)
                if s.exists():
                    after(act, S["max_turned"], s)
                    after(act, S["shifted_made"], s.before(2), 4)
                    copy(max_t[s.slot][:], ps_mt).then_inc(S["max_kept"], 1)
                if i.exists():
                    after(act, S["k_made"], i)
                    after(act, S["k_turned"], i.before(2))
                    copy(k_parts[i.slot][:, :, 0, :, :], twice(ps_k)).then_inc(S["k_hi_done"], 1)
                if p.exists():
                    after(act, S["topv_done"], p)
                    a.activation(kept[:, bass.ds(p.number, 1), 0:2],
                                 top_v[p.slot][:, 0:TOP_K].rearrange("p (a b) -> p a b", a=1),
                                 ACT.Exp, scale=-1.0).then_inc(S["gate_exp"], 1)
                if s.exists():
                    exps(0)
                    exps(2)
                if i.exists():
                    after(act, S["q_turned"], i)
                    after(act, S["shifted_made"], i.before(2), 4)
                    copy(q_t[i.slot][:], ps_qt).then_inc(S["q_kept"], 1)
                if o.exists():
                    after(act, S["rstd2_done"], o)
                    a.activation(kept[:, bass.ds(o.number, 1), 2:4],
                                 mv2[o.slot][:, 0:3:2].rearrange("p (a b) -> p a b", a=1),
                                 ACT.Copy).then_inc(S["norm_kept"], 1)

            for_all_steps(act, BATCHES, 3, step, 4)

            def tile_step(i):
                t, y = i.before(1), i.before(4)
                if i.exists():
                    after(act, S["xe_turned"], i)
                    after(act, S["ge_made"], i.before(2))
                    copy(xe_t[i.slot][:], pe_xe[i.slot]).then_inc(S["xe_kept"], 1)
                if t.exists():
                    after(act, S["ge_made"], t)
                    after(act, S["ge_done"], t.before(2))
                    a.activation(te[t.slot][:], pe_gu[t.slot][:, 0:I], ACT.Tanh, scale=0.5
                                 ).then_inc(S["te_done"], 1)
                if y.exists():
                    after(act, S["ye_done"], y)
                    act.dma_start(rows(ys_dram, y), ye[y.slot][:]).then_inc(ye_out[y.slot], 16)

            for_all_steps(act, TILES, 4, tile_step, 4)

            act.wait_ge(S["gate_done"], 5)

            def last_step(i):
                t, h = i.before(1), i.before(3)
                if i.exists():
                    landed(act, x1_in, i)
                    after(act, S["xn3_done"], i.before(2))
                    a.activation(centred[i.slot][:], x1_back[i.slot4][:], ACT.Identity, bias=of_batch(i, 2)
                                 ).then_inc(S["centred_done"], 1)
                if h.exists():
                    after(act, S["hsh_turned"], h)
                    after(act, S["shared_made"], h.before(2))
                    copy(hsh_t[h.slot][:], pe_h[h.slot]).then_inc(S["hsh_kept"], 1)
                if i.exists():
                    after(act, S["centred_done"], i)
                    after(act, S["xn3_turned"], i.before(2))
                    after(act, S["both_done"], i.before(2))
                    a.activation(xn3[i.slot][:], centred[i.slot][:], ACT.Copy, scale=of_batch(i, 3)
                                 ).then_inc(S["xn3_done"], 1)
                if t.exists():
                    after(act, S["gsh_made"], t)
                    after(act, S["gsh_done"], t.before(2))
                    a.activation(tsh[t.slot][:], pe_gu[t.slot][:, 0:I], ACT.Tanh, scale=0.5
                                 ).then_inc(S["tsh_done"], 1)
                if i.exists():
                    after(act, S["xn3_turned"], i)
                    after(act, S["gsh_made"], i.before(2))
                    copy(xn3_t[i.slot][:], pe_xe[i.slot]).then_inc(S["xn3_kept"], 1)

            for_all_steps(act, BATCHES, 3, last_step, 4)

        @block.vector
        def _(dve):
            v = nc.vector

            def stand(slot):
                v.memset(spare_dve[slot][:], 0.0)

            dve.wait_ge(consts, 1)
            v.tensor_copy(row_iota[:], row_int[:])
            v.tensor_scalar(row_int4[:], row_int[:], 3, None, ALU.bitwise_and).then_inc(setup_v, 1)
            dve.wait_ge(setup_v, 1)
            v.tensor_copy(row_mod4[:], row_int4[:])
            v.tensor_scalar(ident[:], col_iota[:], row_iota[:, 0:1], None, ALU.is_equal)
            v.tensor_scalar(ident_bf[:], col_iota[:], row_iota[:, 0:1], None, ALU.is_equal)
            v.tensor_scalar(ident_half[:], col_iota[:], row_iota[:, 0:1], None, ALU.is_equal)
            v.tensor_scalar(earlier[:], col_iota[:], row_iota[:, 0:1], None,
                            ALU.is_gt).then_inc(setup_v, 1)
            dve.wait_ge(setup_v, 2)
            for c in range(HC):
                v.tensor_scalar(pick[:, c, :], row_mod4[:, 0:1].to_broadcast([P, P]), float(c),
                                None, ALU.is_equal)
            dve.wait_ge(w_in, 16 * 12)
            v.tensor_copy(bv_rep[:], bv_col[:, :].unsqueeze(2).to_broadcast([P, DC, P])).then_inc(setup_p, 1)
            v.tensor_copy(bias_parts[:, 0], bias_row[:]).then_inc(bias_split, 1)
            dve.wait_ge(bias_split, 1)
            v.tensor_tensor(bias_left[:], bias_row[:], bias_parts[:, 0], ALU.subtract).then_inc(bias_split, 1)
            dve.wait_ge(bias_split, 2)
            v.tensor_copy(bias_parts[:, 1], bias_left[:]).then_inc(bias_split, 1)
            dve.wait_ge(bias_split, 3)
            v.tensor_tensor(bias_row[:], bias_left[:], bias_parts[:, 1], ALU.subtract).then_inc(bias_split, 1)
            dve.wait_ge(bias_split, 4)
            v.tensor_copy(bias_parts[:, 2], bias_row[:]).then_inc(bias_split, 1)
            dve.wait_ge(setup_pe, 1)
            v.tensor_copy(attn_bias[:], b4[:, 0:D])
            v.tensor_copy(gate_bias[:], b5[:, 0:E]).then_inc(setup_done, 1)

            def moments(b, stats, mv, ready, done, free):
                after(dve, S[ready], b)
                after(dve, S[free], b.before(2))
                stand(b.slot)
                v.bn_aggr(mv[b.slot][:, 0:2], stats[b.slot][:]).then_inc(S[done], 1)

            def with_eps(b, mv, ve, ready, done, free):
                after(dve, S[ready], b)
                after(dve, S[free], b.before(2))
                v.tensor_scalar_add(ve[b.slot][:], mv[b.slot][:, 1:2], LN_EPS).then_inc(S[done], 1)

            def normalise(b, source, target, mv, ready, done):
                after(dve, ready, b)
                v.tensor_scalar(target[b.slot if len(target) == 2 else b.slot4][:], source[b.slot][:], mv[b.slot][:, 0:1],
                                mv[b.slot][:, 2:3], ALU.subtract, ALU.mult).then_inc(done, 1)

            def normalise_x(b):
                after(dve, S["xc_turned"], b.before(2))
                normalise(b, x_sb, xn, mv1, S["rstd1_done"], S["xn_done"])

            first_batch = Batch(0, 0, BATCHES)
            landed(dve, x_in, first_batch)
            v.bn_stats(stats1[0][:], x_sb[0][:]).then_inc(S["stats1_done"], 1)
            moments(first_batch, stats1, mv1, "stats1_done", "mv1_done", "xn_done")
            with_eps(first_batch, mv1, ve1, "mv1_done", "ve1_done", "rstd1_done")
            normalise_x(first_batch)

            def step(i):
                s, o, p, n = i.before(1), i.before(2), i.before(3), i.before(-1)

                def maxima(pair):
                    after(dve, S["scores_made"], s, 4, pair + 2)
                    after(dve, S["max_lo_done"], s.before(2))
                    v.tensor_reduce(neg_max[s.slot][:, pair:pair + 2, :],
                                    ps_s[:, pair:pair + 2, :].rearrange("p r (c t) -> p r c t", c=HC),
                                    axis=AX.X, op=ALU.max, negate=True).then_inc(S["max_taken"], 1)

                def rest_of(ps, parts, low, hi_done, turned, lo_done):
                    after(dve, hi_done, i)
                    after(dve, turned, i.before(2))
                    hi, lo = ((parts[i.slot][:, :, :, 0, :], parts[i.slot][:, :, :, 1, :]) if low == "inner" else
                              (parts[i.slot][:, :, 0, :, :], parts[i.slot][:, :, 1, :, :]))
                    v.tensor_tensor(lo, ps.rearrange("p (h w) -> p h w", h=H).unsqueeze(2).to_broadcast([P, H, 2, DH]),
                                    hi, ALU.subtract).then_inc(lo_done, 1)

                if s.exists():
                    maxima(0)
                if o.exists():
                    after(dve, S["o_turned"], o)
                    after(dve, S["o_done"], o.before(2))
                    v.reciprocal(o_rec[o.slot][:], ps_o[:, :, :, DH]).then_inc(S["rec_done"], 1)
                if p.exists():
                    after(dve, S["logits_made"], p)
                    after(dve, S["key_done"], p.before(1))
                    v.tensor_tensor(key[p.slot][:], ps_router, gate_bias[:], ALU.add).then_inc(S["biased_done"], 1)
                if o.exists():
                    after(dve, S["rec_done"], o)
                    after(dve, S["ot_made"], o.before(2))
                    v.tensor_tensor(o_sb[o.slot][:].rearrange("p (c r w) -> p c r w", c=HC, r=4),
                                    ps_o[:, :, :, 0:DH], o_rec[o.slot][:].unsqueeze(3).to_broadcast([P, HC, 4, DH]),
                                    ALU.mult).then_inc(S["o_done"], 1)
                if p.exists():
                    after(dve, S["biased_done"], p)
                    v.tensor_scalar_min(key[p.slot][:], key[p.slot][:], SIGMOID_ONE).then_inc(S["key_done"], 1)
                if p.exists():
                    after(dve, S["key_done"], p)
                    after(dve, S["gate_exp"], p.before(2))
                    stand(p.slot)
                    v.max(top_v[p.slot][:], key[p.slot][:]).then_inc(S["topv_done"], 1)
                if s.exists():
                    maxima(2)
                if p.exists():
                    after(dve, S["topv_done"], p)
                    stand(p.slot)
                    v.max_index(top_i[p.slot][:], top_v[p.slot][:], key[p.slot][:]).then_inc(S["topi_done"], 1)
                if s.exists():
                    after(dve, S["max_taken"], s, 2)
                    after(dve, S["max_turned"], s.before(2))
                    v.tensor_copy(max_parts[s.slot][:, :, 0:HC], neg_max[s.slot][:]).then_inc(S["max_hi_done"], 1)
                if p.exists():
                    after(dve, S["topi_done"], p)
                    stand(p.slot)
                    v.tensor_copy(expert_all[:, bass.ds(p.number, 1), :].rearrange("p a b -> p (a b)"),
                                  top_i[p.slot][:, 0:TOP_K]).then_inc(S["expert_done"], 1)
                if s.exists():
                    after(dve, S["max_hi_done"], s)
                    v.tensor_tensor(max_parts[s.slot][:, :, HC:2 * HC], neg_max[s.slot][:],
                                    max_parts[s.slot][:, :, 0:HC], ALU.subtract).then_inc(S["max_lo_done"], 1)
                if n.exists():
                    landed(dve, x_in, n)
                    v.bn_stats(stats1[n.slot][:], x_sb[n.slot][:]).then_inc(S["stats1_done"], 1)
                if p.exists():
                    after(dve, S["expert_done"], p)
                    v.tensor_tensor(chosen[p.slot][:], col_iota[:, 0:E].unsqueeze(1).to_broadcast([P, TOP_K, E]),
                                    expert_all[:, bass.ds(p.number, 1), :].rearrange("p a b -> p (a b)").unsqueeze(2).to_broadcast([P, TOP_K, E]),
                                    ALU.is_equal).then_inc(S["chosen_done"], 1)
                if n.exists():
                    moments(n, stats1, mv1, "stats1_done", "mv1_done", "xn_done")
                if i.exists():
                    rest_of(ps_q, q_parts, "inner", S["q_hi_done"], S["q_turned"], S["q_lo_done"])
                if n.exists():
                    with_eps(n, mv1, ve1, "mv1_done", "ve1_done", "rstd1_done")
                if p.exists():
                    after(dve, S["chosen_done"], p)
                    after(dve, S["seen_done"], p.before(2))
                    v.tensor_tensor(chosen_bf[p.slot][:], chosen[p.slot][:, 0, :], chosen[p.slot][:, 1, :],
                                    ALU.add).then_inc(S["chosen_bf_done"], 1)
                if i.exists():
                    rest_of(ps_k, k_parts, "outer", S["k_hi_done"], S["k_turned"], S["k_lo_done"])
                if o.exists():
                    after(dve, S["wo_made"], o)
                    after(dve, S["x_res_done"], o)
                    after(dve, S["xn2_done"], o.before(2))
                    landed(dve, x1_out, o.before(2))
                    v.tensor_tensor(x1[o.slot][:], ps_wo, x_res[o.slot][:], ALU.add).then_inc(S["x1_done"], 1)
                if n.exists():
                    normalise_x(n)
                if o.exists():
                    after(dve, S["x1_done"], o)
                    v.bn_stats(stats2[o.slot][:], x1[o.slot][:]).then_inc(S["stats2_done"], 1)
                    after(dve, S["norm_kept"], o.before(2))
                    moments(o, stats2, mv2, "stats2_done", "mv2_done", "xn2_done")
                    with_eps(o, mv2, ve2, "mv2_done", "ve2_done", "rstd2_done")
                if i.exists():
                    after(dve, S["k_turned"], i)
                    after(dve, S["shifted_made"], i.before(2), 4)
                    v.tensor_copy(k_t[i.slot][:], ps_kt).then_inc(S["k_kept"], 1)
                if p.exists():
                    after(dve, S["rank_made"], p)
                    v.tensor_tensor(rank[p.slot][:], ps_rank, region_start[:], ALU.add).then_inc(S["rank_done"], 1)
                    after(dve, S["rank_done"], p)
                    v.tensor_tensor(rank2[p.slot][:], chosen[p.slot][:],
                                    rank[p.slot][:, :].unsqueeze(1).to_broadcast([P, TOP_K, E]),
                                    ALU.mult).then_inc(S["rank2_done"], 1)
                if o.exists():
                    after(dve, S["sent"], o.before(4), 32)
                    normalise(o, x1, xn2, mv2, S["rstd2_done"], S["xn2_done"])
                if p.exists():
                    after(dve, S["rank2_done"], p)
                    v.tensor_reduce(slot_all[:, bass.ds(p.number, 1), :].rearrange("p a b -> p (a b)"), rank2[p.slot][:],
                                    axis=AX.X, op=ALU.add).then_inc(S["slotf_done"], 1)
                    after(dve, S["slotf_done"], p)
                    after(dve, S["sent"], p.before(4), 32)
                    stand(p.slot)
                    v.tensor_copy(slot_int[p.slot4][:], slot_all[:, bass.ds(p.number, 1), :].rearrange("p a b -> p (a b)")
                                  ).then_inc(S["slot_done"], 1)

            for_all_steps(dve, BATCHES, 3, step, 4)

            def link(instruction):
                instruction.then_inc(S["table"], 1)
                table[0] += 1
                dve.wait_ge(S["table"], table[0])

            table = [0]
            dve.wait_ge(consts, 2)
            dve.wait_ge(S["counted"], 1)
            across = lambda t: t.unsqueeze(1).to_broadcast([P, TC, E])
            along = lambda t: t.unsqueeze(2).to_broadcast([P, TC, E])
            link(v.tensor_copy(rows_of[:], b5[:, 0:E]))
            link(v.tensor_scalar_add(count_int[:], rows_of[:], float(P - 1)))
            link(v.tensor_scalar(tiles_int[:], count_int[:], P.bit_length() - 1, None, ALU.logical_shift_right))
            link(v.tensor_copy(tiles[:], tiles_int[:]))
            link(v.tensor_tensor_scan(tiles_end[:], ones_e[:], tiles[:], 0.0, ALU.mult, ALU.add))
            v.tensor_scalar_add(final[:], tiles_end[:], -1.0)
            v.tensor_scalar(full[:], rows_of[:], float(P), None, ALU.is_ge)
            link(v.tensor_scalar_add(last_tile[:], tiles_end[:, E - 1:E], -1.0))
            link(v.scalar_tensor_tensor(back[:], tiles[:], float(P), rows_of[:], ALU.mult, ALU.subtract))
            link(v.tensor_tensor(back[:], back[:], full[:], ALU.mult))
            link(v.tensor_scalar(tile_iota[:], tile_iota[:], last_tile[:, 0:1], None, ALU.min))
            link(v.tensor_tensor(per_tile[:, 0], across(tiles_end[:]), along(tile_iota[:]), ALU.is_le))
            v.tensor_tensor(per_tile[:, 1], per_tile[:, 0], across(tiles[:]), ALU.mult)
            link(v.tensor_tensor(per_tile[:, 2], across(final[:]), along(tile_iota[:]), ALU.is_equal))
            link(v.tensor_tensor(per_tile[:, 2], per_tile[:, 2], across(back[:]), ALU.mult))
            link(v.tensor_reduce(sums[:], per_tile[:], axis=AX.X, op=ALU.add))
            v.tensor_copy(table_col[:, 0, :], sums[:, 0, :])
            link(v.scalar_tensor_tensor(sums[:, 2, :], sums[:, 0, :], float(REGION), sums[:, 2, :], ALU.mult, ALU.subtract))
            link(v.tensor_tensor(sums[:, 1, :], tile_iota[:], sums[:, 1, :], ALU.subtract))
            v.scalar_tensor_tensor(table_col[:, 1, :], sums[:, 1, :], float(P), sums[:, 2, :], ALU.mult, ALU.add
                                   ).then_inc(S["table"], 1)
            table[0] += 1
            dve.wait_ge(S["tables_turned"], 1)
            v.tensor_copy(row_tab[:], b7[0:1, 0:TC * P]).then_inc(S["tables_kept"], 1)
            v.tensor_copy(expert_row[:, 3:3 + TILES], b6[0:1, 0:TILES]).then_inc(S["packed_done"], 1)
            dve.wait_ge(S["packed_done"], 1)

            def put_digit(n, into, before, count):
                for w in range(2):
                    first = w * DIGITS + n
                    digit = expert_row[:, first:first + TURN * TURNS].rearrange("p (t f) -> p t f", f=TURN)[:, :, 0]
                    if before is None:
                        m = v.tensor_copy(into[:, :, w], digit)
                    else:
                        m = v.scalar_tensor_tensor(into[:, :, w], before[:, :, w], float(E), digit, ALU.mult, ALU.add)
                m.then_inc(S["packed_done"], 1)
                dve.wait_ge(S["packed_done"], count)

            for n in range(DIGITS - 1, -1, -1):
                put_digit(n, packed[n % 2], None if n == DIGITS - 1 else packed[(n + 1) % 2], 1 + DIGITS - n)
            v.tensor_copy(turn_tab[:], packed[0][:].rearrange("p t w -> p (t w)")).then_inc(S["tables_kept"], 1)
            link(v.tensor_tensor(out_shift[:, 0:E], tiles_end[:], tiles[:], ALU.subtract))
            link(v.scalar_tensor_tensor(out_shift[:, 0:E], out_shift[:, 0:E], float(P), region_start[:], ALU.mult, ALU.subtract))
            v.tensor_copy(edge[:, 0, 0:E], region_start[:])
            v.tensor_copy(jump[:, 0, 0:1], out_shift[:, 0:1])
            v.tensor_copy(jump[:, 1, 0:E], back[:])
            v.tensor_scalar_add(edge[:, 1, 0:E], tiles[:], -1.0)
            link(v.tensor_tensor(jump[:, 0, 1:E], out_shift[:, 1:E], out_shift[:, 0:E - 1], ALU.subtract))
            v.tensor_tensor(jump[:, 0, 1:E], jump[:, 0, 1:E], back[:, 0:E - 1], ALU.subtract)
            dve.wait_ge(S["norm_kept"], BATCHES)
            v.tensor_scalar_mul(kept[:, :, 2], kept[:, :, 2], -1.0).then_inc(S["negated"], 1)
            link(v.scalar_tensor_tensor(edge[:, 1, 0:E], edge[:, 1, 0:E], float(P), region_start[:], ALU.mult, ALU.add))
            dve.wait_ge(S["gate_exp"], BATCHES)
            dve.wait_ge(S["negated"], 1)
            v.tensor_scalar_add(gate_all, gate_all, 1.0).then_inc(S["gate_done"], 1)
            dve.wait_ge(S["gate_done"], 1)
            v.reciprocal(gate_all, gate_all).then_inc(S["gate_done"], 1)
            dve.wait_ge(S["gate_done"], 2)
            v.tensor_tensor(gate_sum[:], gate_all[:, :, 0], gate_all[:, :, 1], ALU.add).then_inc(S["gate_done"], 1)
            dve.wait_ge(S["gate_done"], 3)
            v.reciprocal(gate_sum[:], gate_sum[:]).then_inc(S["gate_done"], 1)
            dve.wait_ge(S["gate_done"], 4)
            v.tensor_tensor(gate_all, gate_all, gate_sum[:].unsqueeze(2).to_broadcast([P, BATCHES, TOP_K]),
                            ALU.mult).then_inc(S["gate_done"], 1)
            dve.wait_ge(S["gate_done"], 5)

            def tile_step(i):
                t, h, d = i.before(1), i.before(2), i.before(3)
                if h.exists():
                    after(dve, S["he_turned"], h)
                    after(dve, S["ye_made"], h.before(2))
                    v.tensor_copy(he_t[h.slot][:], pe_h[h.slot]).then_inc(S["he_kept"], 1)
                if t.exists():
                    after(dve, S["te_done"], t)
                    v.scalar_tensor_tensor(ge[t.slot][:], te[t.slot][:], 1.0, pe_gu[t.slot][:, 0:I],
                                           ALU.add, ALU.mult).then_inc(S["ge_done"], 1)
                    after(dve, S["ge_done"], t)
                    after(dve, S["he_turned"], t.before(2))
                    v.scalar_tensor_tensor(he[t.slot][:], ge[t.slot][:], 0.5, pe_gu[t.slot][:, I:2 * I],
                                           ALU.mult, ALU.mult).then_inc(S["he_done"], 1)
                if d.exists():
                    after(dve, S["ye_made"], d)
                    landed(dve, ye_out, d.before(2))
                    v.tensor_copy(ye[d.slot][:], pe_y[d.slot]).then_inc(S["ye_done"], 1)

            for_all_steps(dve, TILES, 3, tile_step, 4)

            def last_step(i):
                b, t, d = i.before(1), i.before(2), i.before(4)
                if d.exists():
                    landed(dve, first_in, d)
                    after(dve, S["both_done"], d)
                    after(dve, S["part2_done"], d.before(2))
                    v.scalar_tensor_tensor(part[d.slot][:], first[d.slot4][:], of_batch(d, 0), both[d.slot4][:],
                                           ALU.mult, ALU.add).then_inc(S["part_done"], 1)
                if t.exists():
                    after(dve, S["tsh_done"], t)
                    v.scalar_tensor_tensor(gsh[t.slot][:], tsh[t.slot][:], 1.0, pe_gu[t.slot][:, 0:I],
                                           ALU.add, ALU.mult).then_inc(S["gsh_done"], 1)
                if d.exists():
                    landed(dve, second_in, d)
                    after(dve, S["part_done"], d)
                    after(dve, S["total_done"], d.before(2))
                    v.scalar_tensor_tensor(part2[d.slot][:], second[d.slot4][:], of_batch(d, 1), part[d.slot][:],
                                           ALU.mult, ALU.add).then_inc(S["part2_done"], 1)
                if t.exists():
                    after(dve, S["gsh_done"], t)
                    after(dve, S["hsh_turned"], t.before(2))
                    v.scalar_tensor_tensor(hsh[t.slot][:], gsh[t.slot][:], 0.5, pe_gu[t.slot][:, I:2 * I],
                                           ALU.mult, ALU.mult).then_inc(S["hsh_done"], 1)
                if d.exists():
                    after(dve, S["part2_done"], d)
                    after(dve, S["shared_made"], d)
                    landed(dve, total_out, d.before(2))
                    v.tensor_tensor(total[d.slot][:], pe_y[d.slot], part2[d.slot][:], ALU.add
                                    ).then_inc(S["total_done"], 1)
                if b.exists():
                    after(dve, S["xn3_done"], b)
                    after(dve, S["part_done"], b.before(4))
                    v.tensor_tensor(both[b.slot4][:], x1_back[b.slot4][:], xn3[b.slot][:], ALU.add
                                    ).then_inc(S["both_done"], 1)

            for_all_steps(dve, BATCHES, 4, last_step, 4)

        @block.tensor
        def _(pe):
            t = nc.tensor
            t_ = nc.tensor.transpose

            def mm(dst, left, right, first=True, last=True, shared=False):
                return t.matmul(dst, left, right, start=first, stop=last, skip_group_check=shared)

            pe.wait_ge(w_in, 16 * 12)
            pe.wait_ge(setup_p, 1)
            pe.wait_ge(setup_v, 2)
            for c in range(DC):
                mm(b4[:, 0:D], bv_rep[:, c, :], wo_sb[:, c, :], c == 0, False)
            mm(b4[:, 0:D], ones_row[:], wo_b_row[:], False, True)
            mm(b5[:, 0:E], ones_row[:], gate_b_row[:]).then_inc(setup_pe, 1)
            pe.wait_ge(setup_done, 1)
            pe.wait_ge(bias_in, 48)

            def step(i):
                s, o, p = i.before(1), i.before(2), i.before(3)

                def project(dst, w, n, x0, done):
                    for c in range(DC):
                        mm(dst, xc_t[i.slot][:, x0 + c, :], w[:, c, :], c == 0, False)
                    mm(dst, ones3[:], bias3[:, n, :], False, True).then_inc(done, 1)

                def halves(b, r, c):
                    g = slice(64 * (r % 2), 64 * (r % 2) + 64)
                    return q_t[b.slot][g, 2 * c + r // 2, :], k_t[b.slot][g, 2 * c + r // 2, :]

                def scores(b, pair):
                    for c in range(HC):
                        for r in (pair, pair + 1):
                            q, k = halves(b, r, c)
                            m = mm(ps_s[:, r, c * P:(c + 1) * P], q, k)
                            if c == HC - 1:
                                m.then_inc(S["scores_made"], 1)

                if s.exists():
                    after(pe, S["q_kept"], s)
                    after(pe, S["k_kept"], s)
                    after(pe, S["probs_done"], s.before(1), 2)
                    scores(s, 0)
                if p.exists():
                    after(pe, S["xn2_done"], p)
                    after_first(pe, (S["rank_done"], p.before(1)), (S["q_lo_done"], s))
                    for c in range(DC):
                        m = t.transpose(ps_x2[:, c, :], xn2[p.slot4][:, c * P:(c + 1) * P], ident[:])
                    m.then_inc(S["x2_turned"], 1)
                if s.exists():
                    scores(s, 2)
                if i.exists():
                    after(pe, S["xn_done"], i)
                    landed(pe, c_in, i)
                    after(pe, S["k_kept"], s)
                    for c in range(DC):
                        t.transpose(ps_xc[:, c, :], xn[i.slot][:, c * P:(c + 1) * P], ident[:])
                    for c in range(DC):
                        m = t.transpose(ps_xc[:, DC + c, :], c_sb[i.slot][:, c * P:(c + 1) * P], ident[:])
                    m.then_inc(S["xc_turned"], 1)
                if o.exists():
                    after(pe, S["pv_kept"], o)
                    after_first(pe, (S["x2_kept"], p), (S["q_lo_done"], s))
                    for c in range(HC):
                        m = t.transpose(b7[:, c * P:(c + 1) * P], o_un[o.slot][:, c, :], ident[:])
                    m.then_inc(S["o_turned"], 1)
                if p.exists():
                    after(pe, S["x2_kept"], p)
                    after_first(pe, (S["pv_kept"], o), (S["x1_done"], p))
                    for c in range(DC):
                        m = mm(ps_router, xn2_t[p.slot][:, c, :], router_sb[:, c, :], c == 0, c == DC - 1)
                    m.then_inc(S["logits_made"], 1)
                if s.exists():
                    for c in range(DC):
                        m = mm(ps_v, xc_t[s.slot][:, DC + c, :], wv_sb[:, c, :], c == 0, c == DC - 1)
                    m.then_inc(S["v_made"], 1)
                if i.exists():
                    after(pe, S["xc_kept"], i)
                    after_first(pe, (S["o_done"], o), (S["q_lo_done"], s))
                    project(ps_q, wq_sb, 0, 0, S["q_made"])
                if o.exists():
                    after(pe, S["o_done"], o)
                    after_first(pe, (S["v_done"], s), (S["max_kept"], o))
                    for c in range(DC):
                        m = t.transpose(ps_ot[:, c, :], o_sb[o.slot][:, c * P:(c + 1) * P], ident[:])
                    m.then_inc(S["ot_made"], 1)
                if i.exists():
                    project(ps_k, wk_sb, 1, DC, S["k_made"])
                if s.exists():
                    after(pe, S["max_lo_done"], s)
                    after_first(pe, (S["ot_kept"], o), (S["v_done"], s))
                    t.transpose(ps_mt, max_parts[s.slot][:].rearrange("p r j -> p (r j)"), ident_bf[:]
                                ).then_inc(S["max_turned"], 1)
                if o.exists():
                    after(pe, S["ot_kept"], o)
                    after_first(pe, (S["biased_done"], p), (S["pv_kept"], o))
                    for c in range(DC):
                        m = mm(ps_wo, o_t[o.slot][:, c, :], wo_sb[:, c, :], c == 0, c == DC - 1)
                    m.then_inc(S["wo_made"], 1)
                if s.exists():
                    after(pe, S["max_kept"], s)
                    for pair in (0, 2):
                        for c in range(HC):
                            for r in (pair, pair + 1):
                                q, k = halves(s, r, c)
                                mm(ps_s[:, r, c * P:(c + 1) * P], k, q, c == 0, False, True)
                            for r in (pair, pair + 1):
                                g = slice(32 * r, 32 * r + 32)
                                m = mm(ps_s[:, r, c * P:(c + 1) * P], pick[g, c, :], max_t[s.slot][g, :],
                                       False, True, True)
                                if c == HC - 1:
                                    m.then_inc(S["shifted_made"], 1)
                if i.exists():
                    after(pe, S["q_lo_done"], i)
                    after(pe, S["max_kept"], s)
                    for c in range(H // 2):
                        m = t.transpose(ps_qt[:, c, :], q_parts[i.slot][:, 2 * c:2 * c + 2].rearrange(
                            "p h a b w -> p (h a b w)"), ident_half[:])
                    m.then_inc(S["q_turned"], 1)
                if i.exists():
                    after(pe, S["k_lo_done"], i)
                    for c in range(H // 2):
                        m = t.transpose(ps_kt[:, c, :], k_parts[i.slot][:, 2 * c:2 * c + 2].rearrange(
                            "p h a b w -> p (h a b w)"), ident_half[:])
                    m.then_inc(S["k_turned"], 1)
                if p.exists():
                    after(pe, S["chosen_bf_done"], p)
                    after(pe, S["seen_done"], p.before(1))
                    after_first(pe, (S["q_lo_done"], i), (S["o_done"], o), (S["x2_kept"], p))
                    mm(ps_rank, earlier[:], chosen_bf[p.slot][:], True, False)
                    mm(ps_rank, ones_bf[:], seen[:], False, True).then_inc(S["rank_made"], 1)
                if s.exists():
                    after(pe, S["probs_done"], s, 2)
                    after(pe, S["v_done"], s)
                    after_first(pe, (S["x1_done"], o))
                    for c in range(HC):
                        for r in range(4):
                            g = slice(32 * r, 32 * r + 32)
                            m = mm(ps_pv[g, c, :], v_sb[s.slot][:, 4 * c + r, :], probs[s.slot][:, r, c, :])
                    m.then_inc(S["pv_made"], 1)

            for_all_steps(pe, BATCHES, 3, step, 4)

            pe.wait_ge(S["seen_done"], BATCHES)
            pe.wait_ge(S["o_done"], BATCHES)
            pe.wait_ge(S["k_kept"], BATCHES)
            mm(b5[:, 0:E], ones_bf[:], seen[:]).then_inc(S["counted"], 1)
            pe.wait_ge(S["table"], TABLE_STEPS)
            pe.wait_ge(S["pv_kept"], BATCHES)
            pe.wait_ge(S["rank_done"], BATCHES)
            pe.wait_ge(S["biased_done"], BATCHES)
            pe.wait_ge(S["x1_done"], BATCHES)
            for n, table in enumerate((b6, b7)):
                for c in range(TC):
                    m = mm(table[0:1, c * P:(c + 1) * P], table_col[:, n, c:c + 1], ident[:])
            m.then_inc(S["tables_turned"], 1)
            pe.wait_ge(w_in2, 2 * E * 16)
            pe.wait_ge(S["tables_kept"], 2)
            pe.wait_ge(S["max_kept"], BATCHES)

            experts_read = []

            def tile_step(i):
                t, h, d = i.before(1), i.before(2), i.before(3)
                if i.offset % TURN == 0:
                    words = read_registers(mybir.EngineType.PE,
                                           turn_tab[0:1, bass.ds((i.turn + i.offset // TURN) * 2, 2)],
                                           E ** DIGITS - 1)
                    experts_read[:] = [(word >> DIGIT_BITS * n) & (E - 1) for word in words for n in range(DIGITS)]
                e_t, e_d = experts_read[i.offset % TURN + 2], experts_read[i.offset % TURN]
                if i.exists():
                    landed(pe, xe_in, i)
                    after(pe, S["xe_kept"], i.before(2))
                    for c in range(DC):
                        m = t_(pe_xe[i.slot][:, c, :], xe[i.slot4][:, c * P:(c + 1) * P], ident[:])
                    m.then_inc(S["xe_turned"], 1)
                if t.exists():
                    after(pe, S["xe_kept"], t)
                    after(pe, S["he_done"], t.before(2))
                    for c in range(DC):
                        m = mm(pe_gu[t.slot], xe_t[t.slot][:, c, :],
                               eg_sb[:, bass.ds(e_t, 1), c, :].rearrange("p a n -> p (a n)"), c == 0, c == DC - 1)
                    m.then_inc(S["ge_made"], 1)
                if h.exists():
                    after(pe, S["he_done"], h)
                    after(pe, S["he_kept"], h.before(2))
                    t_(pe_h[h.slot], he[h.slot][:], ident[:]).then_inc(S["he_turned"], 1)
                if d.exists():
                    after(pe, S["he_kept"], d)
                    after(pe, S["ye_done"], d.before(2))
                    mm(pe_y[d.slot], he_t[d.slot][:], ed_sb[:, bass.ds(e_d, 1), :].rearrange("p a n -> p (a n)")
                       ).then_inc(S["ye_made"], 1)

            for_all_steps(pe, TILES, 3, tile_step, TURN)

            pe.wait_ge(S["he_done"], TILES)
            pe.wait_ge(S["he_kept"], TILES)
            pe.wait_ge(S["ye_done"], TILES)

            def last_step(i):
                t, h, d = i.before(1), i.before(3), i.before(4)
                if d.exists():
                    after(pe, S["hsh_kept"], d)
                    after(pe, S["total_done"], d.before(2))
                    mm(pe_y[d.slot], hsh_t[d.slot][:], sd_sb[:]).then_inc(S["shared_made"], 1)
                if h.exists():
                    after(pe, S["hsh_done"], h)
                    after(pe, S["hsh_kept"], h.before(2))
                    t_(pe_h[h.slot], hsh[h.slot][:], ident[:]).then_inc(S["hsh_turned"], 1)
                if t.exists():
                    after(pe, S["xn3_kept"], t)
                    after(pe, S["hsh_done"], t.before(2))
                    for c in range(DC):
                        m = mm(pe_gu[t.slot], xn3_t[t.slot][:, c, :], gu_sb[:, c, :], c == 0, c == DC - 1)
                    m.then_inc(S["gsh_made"], 1)
                if i.exists():
                    after(pe, S["xn3_done"], i)
                    after(pe, S["xn3_kept"], i.before(2))
                    for c in range(DC):
                        m = t_(pe_xe[i.slot][:, c, :], xn3[i.slot][:, c * P:(c + 1) * P], ident[:])
                    m.then_inc(S["xn3_turned"], 1)

            for_all_steps(pe, BATCHES, 4, last_step, 4)


def kernel(**inputs):
    import numpy as np
    import concourse.bacc as bacc
    from concourse.bass_utils import run_bass_kernel_spmd

    a = {name: np.asarray(value) for name, value in inputs.items()}
    x = a["x"]
    rows = lambda n: a[n].reshape(1, -1)
    turned = lambda n: np.ascontiguousarray(a[n].T)
    D = x.shape[-1]
    arrays = {
        "x": x.reshape(-1, D), "ctx": a["ctx_1024"].reshape(-1, D),
        "wq_t": turned("L0_xattn_wq_w"), "wq_b": rows("L0_xattn_wq_b"),
        "wk_t": turned("L0_xattn_wk_w"), "wk_b": rows("L0_xattn_wk_b"),
        "wv_t": turned("L0_xattn_wv_w"), "wv_b": np.ascontiguousarray(a["L0_xattn_wv_b"].reshape(-1, P).T),
        "wo_t": turned("L0_xattn_wo_w"), "wo_b": rows("L0_xattn_wo_b"),
        "gate_w": a["L0_ffn_gate_w"], "gate_b": rows("L0_ffn_gate_b"),
        "shared_gu": np.concatenate([a["L0_ffn_shared_wg"], a["L0_ffn_shared_wu"]], axis=1),
        "shared_d": a["L0_ffn_shared_wd"],
        "experts_gu": np.concatenate([a["L0_ffn_experts_wg"], a["L0_ffn_experts_wu"]], axis=2),
        "experts_d": a["L0_ffn_experts_wd"],
    }
    nc = bacc.Bacc("TRN2", target_bir_lowering=False, num_devices=1)
    arrays = {f"in_{name}": np.ascontiguousarray(value) for name, value in arrays.items()}
    operands = [nc.dram_tensor(name, value.shape, fp32, kind="ExternalInput").ap() for name, value in arrays.items()]
    out = nc.dram_tensor("out", (x.shape[0] * x.shape[1], D), fp32, kind="ExternalOutput").ap()
    xattn_moe_kernel(nc, *operands, out)
    result = run_bass_kernel_spmd(nc, [arrays], core_ids=[0])
    return result.results[0]["out"].reshape(x.shape)
```
